# Optimizing a Trainium2 kernel written in Bass

```python
import numpy as np
import jax
import jax.numpy as jnp

def _softmax(x, axis=-1):
    return jax.nn.softmax(x, axis=axis)

def _gelu(x):
    return jax.nn.gelu(x, approximate=True)

def _silu(x):
    return jax.nn.silu(x)

def _sigmoid(x):
    return jax.nn.sigmoid(x)

def _layernorm(x, axis=-1, eps=1e-05):
    m = jnp.mean(x, axis=axis, keepdims=True)
    v = jnp.var(x, axis=axis, keepdims=True)
    return (x - m) / jnp.sqrt(v + eps)

def _scatter_add(tgt, idx, src, axis=0):
    return tgt.at[idx].add(src)

def _segment_sum(src, seg, n):
    return jax.ops.segment_sum(src, seg, n)
kernel_name = 'mk_xattn_ffn_d1_seqx_r8_200a4c'

def setup_inputs(seed: int=0):
    np.random.seed(seed)
    _w = jnp.asarray

    def _rec_inputs():
        import jax
        import jax.numpy as jnp
        _rk = jax.random.key(seed)
        x = -0.0002928 + 1 * jax.random.normal(jax.random.fold_in(_rk, 1), (4, 256, 128), jnp.float32)
        _lenS = 256 - jax.random.randint(jax.random.fold_in(_rk, 7), (4,), 0, max(1, 256 // 4) + 1, jnp.int32)
        _lenS2 = 256 - jax.random.randint(jax.random.fold_in(_rk, 8), (4,), 0, max(1, 256 // 4) + 1, jnp.int32)
        _ctx_1024P = jax.random.normal(jax.random.fold_in(_rk, 11), (4, 16, 128), jnp.float32)
        _ctx_1024c = jax.random.dirichlet(jax.random.fold_in(_rk, 511), 0.3 * jnp.ones((16,), jnp.float32), (4, 256))
        _ctx_1024t = jnp.einsum('bsk,bkd->bsd', _ctx_1024c, _ctx_1024P)
        _ctx_1024t = _ctx_1024t * jax.lax.rsqrt(jnp.mean(jnp.square(_ctx_1024t)) + 1e-12) * 0.953939
        ctx_1024 = -1.39393e-06 + 0.999914 * (_ctx_1024t + 0.3 * jax.random.normal(jax.random.fold_in(_rk, 611), (4, 256, 128), jnp.float32))
        return (x, ctx_1024)
    x, ctx_1024 = _rec_inputs()

    def _L0_xattn_setup():
        import jax, jax.numpy as jnp
        import numpy as np
        N_HEAD = 16
        MAX_SEQ_LEN = 256
        RATIO = 1
        NEG_INF = -jnp.inf

        def make_alibi_bias(n_head: int, max_seq_len: int, ratio: int) -> jnp.ndarray:
            s = jnp.arange(max_seq_len)[None, :] * ratio
            t = jnp.arange(max_seq_len * ratio)[:, None]
            bias = (s - t).astype(jnp.float32)
            bias = jnp.where(bias > 0, NEG_INF, bias)
            m = jnp.cumprod(jnp.full((n_head,), 2.0 ** (-8.0 / n_head), dtype=jnp.float32))
            return bias[None, :, :] * m[:, None, None]
        key = jax.random.key(seed)
        kq, kk, kv = jax.random.split(key, 3)
        B, T, D = (2, 256, 128)
        return {'q': jax.random.normal(kq, (B, T, D), dtype=jnp.float32), 'k': jax.random.normal(kk, (B, T, D), dtype=jnp.float32), 'v': jax.random.normal(kv, (B, T, D), dtype=jnp.float32)}
    _L0_xattn_all = _L0_xattn_setup()
    _L0_xattn_in = {k: v for k, v in _L0_xattn_all.items() if k in ()}
    del _L0_xattn_all

    def _L0_ffn_setup():
        import jax, jax.numpy as jnp
        import numpy as np
        HIDDEN = 128
        FFN = 512
        NUM_EXPERTS = 8
        TOP_K = 2
        BATCH, SEQ = (2, 256)
        key = jax.random.key(seed)
        ks = jax.random.split(key, 6)
        s_h = 1.0 / np.sqrt(HIDDEN)
        s_f = 1.0 / np.sqrt(FFN)
        return {'hidden_states': jax.random.normal(ks[0], (BATCH, SEQ, HIDDEN), jnp.float32), 'gate_w': jax.random.uniform(ks[1], (HIDDEN, NUM_EXPERTS), jnp.float32, -s_h, s_h), 'gate_b': jax.random.uniform(ks[2], (NUM_EXPERTS,), jnp.float32, -s_h, s_h), 'w1': jax.random.uniform(ks[3], (NUM_EXPERTS, HIDDEN, FFN), jnp.float32, -s_h, s_h), 'w3': jax.random.uniform(ks[4], (NUM_EXPERTS, HIDDEN, FFN), jnp.float32, -s_h, s_h), 'w2': jax.random.uniform(ks[5], (NUM_EXPERTS, FFN, HIDDEN), jnp.float32, -s_f, s_f)}
    _L0_ffn_all = _L0_ffn_setup()
    _L0_ffn_in = {k: v for k, v in _L0_ffn_all.items() if k in ('gate_w', 'gate_b', 'w1', 'w3', 'w2')}
    del _L0_ffn_all
    return {'x': x, 'ctx_1024': ctx_1024, 'L0_ffn_gate_w': _L0_ffn_in['gate_w'], 'L0_ffn_gate_b': _L0_ffn_in['gate_b'], 'L0_ffn_w1': _L0_ffn_in['w1'], 'L0_ffn_w3': _L0_ffn_in['w3'], 'L0_ffn_w2': _L0_ffn_in['w2']}

def reference(x, ctx_1024, L0_ffn_gate_w, L0_ffn_gate_b, L0_ffn_w1, L0_ffn_w3, L0_ffn_w2):
    import jax
    import jax.numpy as jnp

    def _L0_xattn_ref(q, k, v):
        import jax, jax.numpy as jnp
        import numpy as np
        N_HEAD = 16
        MAX_SEQ_LEN = 256
        RATIO = 1
        NEG_INF = -jnp.inf

        def make_alibi_bias(n_head: int, max_seq_len: int, ratio: int) -> jnp.ndarray:
            s = jnp.arange(max_seq_len)[None, :] * ratio
            t = jnp.arange(max_seq_len * ratio)[:, None]
            bias = (s - t).astype(jnp.float32)
            bias = jnp.where(bias > 0, NEG_INF, bias)
            m = jnp.cumprod(jnp.full((n_head,), 2.0 ** (-8.0 / n_head), dtype=jnp.float32))
            return bias[None, :, :] * m[:, None, None]
        B, T, D = q.shape
        S = k.shape[1]
        H = N_HEAD
        dh = D // H
        qh = q.reshape(B, T, H, dh).transpose(0, 2, 1, 3)
        kh = k.reshape(B, S, H, dh).transpose(0, 2, 1, 3)
        vh = v.reshape(B, S, H, dh).transpose(0, 2, 1, 3)
        scores = jnp.einsum('bhtd,bhsd->bhts', qh, kh) / jnp.sqrt(jnp.float32(dh))
        bias = make_alibi_bias(H, MAX_SEQ_LEN, RATIO)[:, -T:, -S:]
        attn = jax.nn.softmax(scores + bias[None], axis=-1)
        out = jnp.einsum('bhts,bhsd->bhtd', attn, vh)
        return out.transpose(0, 2, 1, 3).reshape(B, T, D)

    def _L0_ffn_ref(hidden_states, gate_w, gate_b, w1, w3, w2):
        import jax, jax.numpy as jnp
        import numpy as np
        HIDDEN = 128
        FFN = 512
        NUM_EXPERTS = 8
        TOP_K = 2
        BATCH, SEQ = (2, 256)
        B, S, D = hidden_states.shape
        T = B * S
        x = hidden_states.reshape(T, D)
        logits = x @ gate_w + gate_b
        probs = jax.nn.softmax(logits.astype(jnp.float32), axis=-1)
        top_w, top_idx = jax.lax.top_k(probs, TOP_K)
        top_w = top_w / jnp.sum(top_w, axis=-1, keepdims=True)
        combine = jnp.zeros((T, NUM_EXPERTS), jnp.float32)
        combine = combine.at[jnp.arange(T)[:, None], top_idx].set(top_w)
        combine = combine.astype(x.dtype)
        h = jax.nn.silu(jnp.einsum('td,edf->tef', x, w1)) * jnp.einsum('td,edf->tef', x, w3)
        out_e = jnp.einsum('tef,efd->ted', h, w2)
        out = jnp.einsum('ted,te->td', out_e, combine)
        return out.reshape(B, S, D)
    x = x + _L0_xattn_ref(_layernorm(x, axis=-1), ctx_1024, ctx_1024)
    x = x + _L0_ffn_ref(_layernorm(x, axis=-1), L0_ffn_gate_w, L0_ffn_gate_b, L0_ffn_w1, L0_ffn_w3, L0_ffn_w2)
    return x

_drawn_inputs = setup_inputs


def setup_inputs(seed=0):
    import zlib

    import numpy as np

    out = dict(_drawn_inputs(seed))
    spreads = {}
    factors = {'L0_ffn_gate_b': 4.325}
    for name, (base, spread) in spreads.items():
        noise = np.random.default_rng([zlib.crc32(name.encode()), seed]).standard_normal(out[name].shape)
        drawn = base * np.exp(spread * noise) if base else spread * noise
        out[name] = jnp.asarray(drawn.astype(out[name].dtype))
    for name, factor in factors.items():
        out[name] = (out[name] * factor).astype(out[name].dtype)
    return out
```

```python
from contextlib import ExitStack

import numpy as np
import concourse.bass as bass
from concourse import mybir

P = 128
BATCH, SEQ, D = 4, 256, 128
HEADS, HEAD_DIM = 16, 8
EXPERTS, FFN, TOP_K = 8, 512, 2
EPS = 1e-5

TILES = BATCH * SEQ // P
TPB = SEQ // P
GROUPS = HEADS // 4
ROWS = 32
QK_COLS = 3 * HEAD_DIM
MAX_COL = QK_COLS + 4
VCOLS = HEAD_DIM + 1
HALF = HEADS // 2
VROWS = HALF * VCOLS
SCORE_COLS = SEQ + P
FT = FFN // P
TOKENS = BATCH * SEQ
CHUNK = 512
CHUNKS = TOKENS // CHUNK
UNITS = 2 * CHUNKS * FT
LAG = 3


def constants():
    def high(a):
        bits = np.ascontiguousarray(a, np.float32).view(np.uint32).astype(np.uint64)
        return ((bits + 0x800) & 0xFFFFF000).astype(np.uint32).view(np.float32)

    slope = np.cumprod(np.full(HEADS, 2.0 ** (-8.0 / HEADS), np.float32), dtype=np.float32)
    token = np.arange(SEQ, dtype=np.float32).reshape(TPB, P).T[:, :, None]
    q = np.zeros((P, TPB, HEADS, 8), np.float32)
    k = np.zeros((P, TPB, HEADS, 8), np.float32)
    down = (-token * slope).astype(np.float32)
    q[..., 0], q[..., 1] = high(slope), slope - high(slope)
    q[..., 2], q[..., 3] = high(down), down - high(down)
    k[..., 0] = k[..., 1] = token
    k[..., 2:6] = 1.0
    p = np.arange(P)
    return np.concatenate([np.eye(P), np.where(p[None, :] > p[:, None], -1e30, 0.0),
                           np.where(p[:, None] > p[None, :], -1e30, 0.0),
                           q.reshape(P, -1), k.reshape(P, -1)], 1).astype(np.float32)


def build(nc, x, ctx_in, gate_w, gate_b, w1, w3, w2, consts, out, c_dram):
    F32, F32R, BF16 = mybir.dt.float32, mybir.dt.float32r, mybir.dt.bfloat16
    ALU, ACT, AX = mybir.AluOpType, mybir.ActivationFunctionType, mybir.AxisListType
    ds = bass.ds

    with ExitStack() as stack:
        def sb(name, shape, dt=F32):
            return stack.enter_context(nc.sbuf_tensor(name, shape, dt))

        def sem(name):
            return stack.enter_context(nc.semaphore(name))

        cf = sb("cf", [P, 3 * P + 2 * TPB * HEADS * 8])
        ident = cf[:, 0:P]
        q_const = cf[:, 3 * P:3 * P + TPB * HEADS * 8].rearrange("p (n c) -> p n c", c=8)
        k_const = cf[:, 3 * P + TPB * HEADS * 8:].rearrange("p (n c) -> p n c", c=8)
        cb = sb("cb", [P, 3, P], BF16)
        x_in = sb("x_in", [P, TILES, D])
        k_in = sb("k_in", [P, TPB, D])
        v_in = sb("v_in", [P, TPB, D])
        gate_sb = sb("gate_sb", [P, EXPERTS])
        bias_sb = sb("bias_sb", [P, EXPERTS])
        w1_sb = sb("w1_sb", [P, EXPERTS * FFN])
        w3_sb = sb("w3_sb", [P, EXPERTS * FFN])
        w2_sb = sb("w2_sb", [P, EXPERTS * FFN])
        bn = sb("bn", [P, TILES, 6])
        stats = sb("stats", [P, TILES * 2])
        veps = sb("veps", [P, TILES])
        std = sb("std", [P, TILES])
        rstd = sb("rstd", [P, TILES])
        rstd_q = sb("rstd_q", [P, TILES])
        q_norm = sb("q_norm", [P, TPB, D])
        q_nat = sb("q_nat", [P, TPB * HEADS, ROWS])
        k_nat = sb("k_nat", [P, TPB * HEADS, ROWS])
        qk_t = sb("qk_t", [P, GROUPS, 2, SEQ], F32R)
        q_max_t = sb("q_max_t", [P, GROUPS, SEQ], F32R)
        neg_max = sb("neg_max", [P, TPB, 4])
        max_nat = sb("max_nat", [P, TPB, 4, ROWS])
        zeros = sb("zeros", [P, TPB * D])
        v_pad = sb("v_pad", [P, TPB * HEADS * VROWS + HALF * VCOLS])
        probs = [sb(f"probs{i}", [P, 2, SCORE_COLS]) for i in range(2)]
        o_t = sb("o_t", [VROWS, 2, SEQ])
        r_den = sb("r_den", [P, TPB, HALF])
        attn = sb("attn", [P, TPB, HALF, HEAD_DIM])
        x_mid = sb("x_mid", [P, TILES, D])
        x_norm = sb("x_norm", [P, TILES, D])
        xh = sb("xh", [P, TOKENS], F32R)
        xl = sb("xl", [P, TOKENS], F32R)
        gate_hl = sb("gate_hl", [P, 2, EXPERTS], F32R)
        logits = sb("logits", [P, TILES, EXPERTS])
        row = sb("row", [P, TILES])
        prob = sb("prob", [P, TILES, EXPERTS])
        top = sb("top", [P, TILES, 8])
        rest = sb("rest", [P, TILES, EXPERTS])
        comb = sb("comb", [P, EXPERTS, TILES])
        comb_t = sb("comb_t", [EXPERTS * TILES, P])
        comb_all = [sb(f"comb_all{i}", [P, TOKENS]) for i in range(2)]
        wh = [[sb(f"wh{m}_{i}", [P, FFN], F32R) for m in range(3)] for i in range(2)]
        wl = [[sb(f"wl{m}_{i}", [P, FFN], F32R) for m in range(3)] for i in range(2)]
        silu = [sb(f"silu{i}", [P, CHUNK]) for i in range(2)]
        hid = [sb(f"hid{i}", [P, CHUNK]) for i in range(2)]
        hh = [sb(f"hh{i}", [P, CHUNK], F32R) for i in range(4)]
        hl = [sb(f"hl{i}", [P, CHUNK], F32R) for i in range(4)]
        part = [sb(f"part{i}", [P, CHUNK]) for i in range(2)]
        acc = sb("acc", [P, CHUNKS, CHUNK])
        y = sb("y", [P, TILES, D])

        banks = stack.enter_context(nc.psum_tensor("banks", [P, 8, 512], F32))
        s1 = banks[:, 0:2]
        s2 = [banks[:, 2:4], banks[:, 4:6]]
        pv = banks[:, 6]
        misc = banks[:, 7]
        g_ps = [banks[:, 0], banks[:, 1]]
        u_ps = [banks[:, 2], banks[:, 3]]
        d_ps = [banks[:, 4], banks[:, 5]]

        def diagonal(bank):
            return bank.rearrange("p (a b) -> p a b", b=SEQ)[:, :, 0:P]

        const_in = sem("const_in")
        first_in = sem("first_in")
        k_loaded = sem("k_loaded")
        v_loaded = sem("v_loaded")
        rest_in = sem("rest_in")
        gate_in = sem("gate_in")
        w_in = sem("w_in")
        comb_out = sem("comb_out")
        comb_in = [sem(f"comb_in{i}") for i in range(2)]
        out_sem = sem("out_sem")
        dve_chain = sem("dve_chain")
        pool_chain = sem("pool_chain")
        masks_ready = sem("masks_ready")
        var_ready = sem("var_ready")
        std_ready = sem("std_ready")
        q_nat_ready = sem("q_nat_ready")
        k_nat_ready = sem("k_nat_ready")
        v_ready = [sem(f"v_ready{i}") for i in range(2)]
        stacked = sem("stacked")
        stack_kept = sem("stack_kept")
        s1_done = [sem(f"s1_done{i}") for i in range(2)]
        max_done = [sem(f"max_done{i}") for i in range(2)]
        max_split = sem("max_split")
        max_turned = sem("max_turned")
        q_max_ready = sem("q_max_ready")
        s2_done = [sem(f"s2_done{i}") for i in range(2)]
        exp_done = [sem(f"exp_done{i}") for i in range(2)]
        pv_done = [sem(f"pv_done{i}") for i in range(2)]
        pv_kept = [sem(f"pv_kept{i}") for i in range(2)]
        pv_turned = [sem(f"pv_turned{i}") for i in range(2)]
        attn_done = [sem(f"attn_done{i}") for i in range(2)]
        var2_ready = sem("var2_ready")
        std2_ready = sem("std2_ready")
        x_norm_ready = sem("x_norm_ready")
        x_turned = sem("x_turned")
        xh_ready = sem("xh_ready")
        xl_ready = sem("xl_ready")
        gate_ready = sem("gate_ready")
        logits_done = sem("logits_done")
        shifted = sem("shifted")
        gate_exp = sem("gate_exp")
        comb_ready = sem("comb_ready")
        comb_turned = sem("comb_turned")
        comb_kept = sem("comb_kept")
        w_high = sem("w_high")
        w_split = [sem(f"w_split{i}") for i in range(2)]
        up_done = sem("up_done")
        silu_done = [sem(f"silu_done{i}") for i in range(2)]
        mul_done = [sem(f"mul_done{i}") for i in range(2)]
        hh_done = [sem(f"hh_done{i}") for i in range(4)]
        hl_done = [sem(f"hl_done{i}") for i in range(4)]
        down_done = [sem(f"down_done{i}") for i in range(4)]
        scaled = [sem(f"scaled{i}") for i in range(2)]
        summed = [sem(f"summed{i}") for i in range(2)]
        y_turned = sem("y_turned")
        y_ready = sem("y_ready")

        def after(n):
            return n + 1

        block = stack.enter_context(nc.Block())

        LAST = BATCH - 1
        PAIRS = EXPERTS // 2

        @block.sync
        def _(sp):
            tiled = lambda a: a.rearrange("(n p) d -> p n d", p=P)
            sp.dma_start(x_in[:, 0:TPB], tiled(x)[:, 0:TPB]).then_inc(first_in, 16)
            sp.dma_start(k_in[:], tiled(ctx_in)[:, 0:TPB]).then_inc(k_loaded, 16)
            sp.dma_start(v_in[:], tiled(ctx_in)[:, 0:TPB]).then_inc(v_loaded, 16)
            sp.dma_start(x_in[:, TPB:], tiled(x)[:, TPB:]).then_inc(rest_in, 16)
            sp.dma_start(gate_sb[:], gate_w).then_inc(gate_in, 16)
            sp.dma_start(bias_sb[:], gate_b.partition_broadcast(P)).then_inc(gate_in, 16)
            sp.dma_start(w1_sb[:].rearrange("p (e f) -> p e f", e=EXPERTS),
                         w1.rearrange("e d f -> d e f")).then_inc(w_in, 16)
            sp.dma_start(w3_sb[:].rearrange("p (e f) -> p e f", e=EXPERTS),
                         w3.rearrange("e d f -> d e f")).then_inc(w_in, 16)
            sp.dma_start(w2_sb[:].rearrange("p (n d) -> p n d", d=D),
                         tiled(w2)).then_inc(w_in, 16)
            with sp.Fori(1, BATCH) as b:
                sp.wait_ge(k_nat_ready, b)
                sp.dma_start(k_in[:], tiled(ctx_in)[:, ds(TPB * b, TPB)]).then_inc(k_loaded, 16)
                sp.wait_ge(v_ready[0], b)
                sp.wait_ge(v_ready[1], b)
                sp.dma_start(v_in[:], tiled(ctx_in)[:, ds(TPB * b, TPB)]).then_inc(v_loaded, 16)
            sp.wait_ge(comb_kept, 1)
            sp.dma_start(c_dram, comb_t[:]).then_inc(comb_out, 16)
            sp.wait_ge(comb_out, 16)
            rows = c_dram.rearrange("(e n) t -> e (n t)", e=EXPERTS)
            def load_comb(i, e):
                sp.dma_start(comb_all[i][:], rows[ds(e, 1), :].rearrange("a t -> (a t)")
                             .partition_broadcast(P)).then_inc(comb_in[i], 16)

            for i in range(2):
                load_comb(i, i)
            with sp.Fori(1, PAIRS) as pair:
                for i in range(2):
                    for c in range(CHUNKS):
                        sp.wait_ge(scaled[c], after(2 * pair + (i - 1)))
                    load_comb(i, 2 * pair + i)
            flat = tiled(out)
            half = TILES // 2
            for c in range(2):
                sp.wait_ge(y_ready, c + 1)
                sp.dma_start(flat[:, c * half:(c + 1) * half],
                             y[:, c * half:(c + 1) * half]).then_inc(out_sem, 16)
            sp.wait_ge(out_sem, 32)

        @block.tensor
        def _(pe):
            for s in (*pv_done, *pv_turned, up_done, *down_done):
                pe.sem_inc(s, 1)

            def stack_group(g):
                for nat, at in ((q_nat, 0), (k_nat, SEQ)):
                    for t in range(TPB):
                        src = nat[:, t * HEADS + 4 * g:t * HEADS + 4 * g + 4, :]
                        last = nc.tensor.transpose(misc[:, at + t * P:at + (t + 1) * P],
                                                   src.rearrange("p h r -> p (h r)"), ident)
                last.then_inc(stacked, 1)

            def scores(g, half, banks_, queries_on_partitions):
                mask = cb[:, 1 if queries_on_partitions else 2, :]
                for j in range(2):
                    nc.tensor.matmul(diagonal(banks_[:, j]), cb[:, 0, :],
                                     mask.unsqueeze(1).broadcast_to([P, 2, P]),
                                     start=True, stop=False, skip_group_check=True)
                for j in range(2):
                    r = ROWS * (2 * half + j)
                    q1 = qk_t[r:r + ROWS, g, 0, :]
                    k1 = qk_t[r:r + ROWS, g, 1, :]
                    q2 = q_max_t[r:r + ROWS, g, :]
                    b = banks_[:, j]
                    if queries_on_partitions:
                        nc.tensor.matmul(b[:, 0:P], q1[:, 0:P], k1[:, 0:P],
                                         start=False, stop=False, skip_group_check=True)
                        last = nc.tensor.matmul(b[:, P:P + SEQ], q1[:, P:SEQ], k1[:, 0:SEQ],
                                                start=False, stop=True, skip_group_check=True)
                    else:
                        nc.tensor.matmul(b[:, 0:SEQ], k1[:, 0:P], q2[:, 0:SEQ],
                                         start=False, stop=False, skip_group_check=True)
                        last = nc.tensor.matmul(b[:, SEQ:SEQ + P], k1[:, P:SEQ], q2[:, P:SEQ],
                                                start=False, stop=True, skip_group_check=True)
                return last

            def values(g, half, j):
                h = 4 * g + 2 * half + j
                grp, first, final = h // HALF, h % HALF == 0, h % HALF == HALF - 1
                acc_ = pv[0:VROWS, grp * SEQ:(grp + 1) * SEQ]
                p_ = probs[half][:, j, :]
                own = [v_pad[:, (t * HEADS + h) * VROWS:(t * HEADS + h + 1) * VROWS]
                       for t in range(TPB)]
                nc.tensor.matmul(acc_, own[0], p_[:, 0:SEQ], start=first, stop=False,
                                 skip_group_check=True)
                return nc.tensor.matmul(acc_[:, P:SEQ], own[1], p_[:, SEQ:SEQ + P],
                                        start=False, stop=final, skip_group_check=True)

            def turn_max():
                for t in range(TPB):
                    last = nc.tensor.transpose(misc[:, t * P:(t + 1) * P],
                                               max_nat[:, t].rearrange("p h r -> p (h r)"), ident)
                last.then_inc(max_turned, 1)

            def turn_values(grp):
                for t in range(TPB):
                    last = nc.tensor.transpose(misc[:, t * VROWS:(t + 1) * VROWS],
                                               o_t[:, grp, t * P:(t + 1) * P],
                                               ident[0:VROWS, 0:VROWS])
                last.then_inc(pv_turned[grp], 1)

            pe.wait_ge(const_in, 16)
            pe.wait_ge(masks_ready, 1)
            pe.wait_ge(q_nat_ready, 1)
            pe.wait_ge(k_nat_ready, 1)
            for g in range(GROUPS):
                pe.wait_ge(stack_kept, g)
                stack_group(g)
            pe.wait_ge(stack_kept, 1)
            for half in range(2):
                if half:
                    pe.wait_ge(max_done[0], 1)
                scores(0, half, s1, True).then_inc(s1_done[half], 1)
            pe.wait_ge(stack_kept, GROUPS)
            pe.wait_ge(max_split, 1)
            turn_max()

            def sequence(b, last_one):
                for g in range(GROUPS):
                    n = 4 * b + g
                    ahead = not (last_one and g == GROUPS - 1)
                    nxt = (g + 1) % GROUPS
                    pe.wait_ge(q_max_ready, n + 1)
                    for half in range(2):
                        pe.wait_ge(exp_done[half], after(n))
                        scores(g, half, s2[half], False).then_inc(s2_done[half], 1)
                    if ahead:
                        pe.wait_ge(max_done[1], n + 1)
                        pe.wait_ge(stack_kept, n + 2)
                        scores(nxt, 0, s1, True).then_inc(s1_done[0], 1)
                    pe.wait_ge(exp_done[0], after(n + 1))
                    if g % 2 == 0:
                        pe.wait_ge(v_ready[g // 2], b + 1)
                        pe.wait_ge(pv_kept[g // 2], after(b))
                    values(g, 0, 0)
                    if ahead:
                        pe.wait_ge(max_done[0], n + 2)
                        scores(nxt, 1, s1, True).then_inc(s1_done[1], 1)
                    values(g, 0, 1).then_inc(pv_done[0], 1)
                    pe.wait_ge(exp_done[1], after(n + 1))
                    values(g, 1, 0)
                    if ahead:
                        pe.wait_ge(max_split, n + 2)
                        if not last_one:
                            pe.wait_ge(stack_kept, n + GROUPS)
                        if g == 0:
                            pe.wait_ge(attn_done[1], after(b))
                        if g == GROUPS - 1 or last_one:
                            pe.wait_ge(attn_done[0], after(b + (1 if g == GROUPS - 1 else 0)))
                        turn_max()
                    values(g, 1, 1).then_inc(pv_done[1], 1)
                    if not last_one:
                        if g == 0:
                            pe.wait_ge(q_nat_ready, b + 2)
                            pe.wait_ge(k_nat_ready, b + 2)
                        pe.wait_ge(q_max_ready, n + 2)
                        stack_group(g)
                    if g >= 2:
                        grp = g - 2
                        pe.wait_ge(pv_kept[grp], after(b + 1))
                        if last_one:
                            if ahead:
                                pe.wait_ge(q_max_ready, n + 2)
                            else:
                                pe.wait_ge(attn_done[0], after(b + 1))
                        else:
                            pe.wait_ge(stack_kept, n + GROUPS + 1)
                        turn_values(grp)

            with pe.Fori(0, LAST) as b:
                sequence(b, False)
            sequence(LAST, True)

            for t in range(TILES):
                if t % (TILES // 2) == 0:
                    pe.wait_ge(x_norm_ready, 1 + t // (TILES // 2))
                last = nc.tensor.transpose(d_ps[t // 4][:, (t % 4) * P:(t % 4 + 1) * P],
                                           x_norm[:, t, :], ident)
                if t % 4 == 3:
                    last.then_inc(x_turned, 1)
            pe.wait_ge(xl_ready, 2)
            pe.wait_ge(gate_ready, 1)

            def gate():
                for t in range(TILES):
                    o = pv[:, t * EXPERTS:(t + 1) * EXPERTS]
                    at = slice(t * P, (t + 1) * P)
                    nc.tensor.matmul(o, xh[:, at], gate_hl[:, 0, :], start=True, stop=False)
                    nc.tensor.matmul(o, xh[:, at], gate_hl[:, 1, :], start=False, stop=False)
                    last = nc.tensor.matmul(o, xl[:, at], gate_hl[:, 0, :], start=False, stop=True)
                last.then_inc(logits_done, 1)

            def up(k, base, pair):
                i, c, j = k // (CHUNKS * FT) % 2, k // FT % CHUNKS, k % FT
                n = k % UNITS
                turn = base + k // 2
                if c == 0 and j == 0:
                    pe.wait_ge(w_split[i], 3 * (pair + k // UNITS) + 1)
                xs = slice(c * CHUNK, (c + 1) * CHUNK)
                js = slice(j * P, (j + 1) * P)
                for m, ps in ((0, g_ps[n % 2]), (1, u_ps[n % 2])):
                    if m == 0:
                        pe.wait_ge(silu_done[n % 2], after(turn))
                    else:
                        if c == 0 and j == 0:
                            pe.wait_ge(w_split[i], 3 * (pair + k // UNITS) + 2)
                        pe.wait_ge(mul_done[n % 2], after(turn))
                    nc.tensor.matmul(ps, wh[i][m][:, js], xh[:, xs], start=True, stop=False)
                    nc.tensor.matmul(ps, wh[i][m][:, js], xl[:, xs], start=False, stop=False)
                    last = nc.tensor.matmul(ps, wl[i][m][:, js], xh[:, xs], start=False, stop=True)
                last.then_inc(up_done, 1)

            def down(k, pair):
                i, c, j = k // (CHUNKS * FT), k // FT % CHUNKS, k % FT
                if j == 0:
                    pe.wait_ge(scaled[c], after(2 * pair + i))
                    if c == 0:
                        pe.wait_ge(w_split[i], 3 * pair + 3)
                pe.wait_ge(hl_done[k % 4], after(UNITS // 4 * pair + k // 4 + 1))
                js = slice(j * P, (j + 1) * P)
                h, l = hh[k % 4][:], hl[k % 4][:]
                nc.tensor.matmul(d_ps[c], wh[i][2][:, js], h, start=j == 0, stop=False)
                nc.tensor.matmul(d_ps[c], wh[i][2][:, js], l, start=False, stop=False)
                nc.tensor.matmul(d_ps[c], wl[i][2][:, js], h, start=False,
                                 stop=j == FT - 1).then_inc(down_done[k % 4], 1)

            def turn_comb():
                pe.wait_ge(comb_ready, 1)
                nc.tensor.transpose(misc[0:EXPERTS * TILES, 0:P],
                                    comb[:].rearrange("p e t -> p (e t)"), ident)\
                    .then_inc(comb_turned, 1)

            gate()
            for k in range(LAG):
                up(k, 0, 0)
            turn_comb()
            with pe.Fori(0, PAIRS - 1) as pair:
                for k in range(UNITS):
                    up(k + LAG, UNITS // 2 * pair, pair)
                    down(k, pair)
            pair = PAIRS - 1
            for k in range(UNITS):
                if k + LAG < UNITS:
                    up(k + LAG, UNITS // 2 * pair, pair)
                down(k, pair)
            for c in range(CHUNKS):
                pe.wait_ge(summed[c], after(EXPERTS))
                for t in range(CHUNK // P):
                    last = nc.tensor.transpose(banks[:, 6 + c, t * P:(t + 1) * P],
                                               acc[:, c, t * P:(t + 1) * P], ident)
                last.then_inc(y_turned, 1)

        @block.scalar
        def _(act):
            for s in (*exp_done, *pv_kept, *silu_done):
                act.sem_inc(s, 1)

            act.dma_start(cf[:], consts).then_inc(const_in, 16)
            act.wait_ge(var_ready, 1)
            nc.scalar.activation(std[:], veps[:], ACT.Sqrt).then_inc(std_ready, 1)

            def keep_stack(g, count):
                act.wait_ge(stacked, count)
                nc.scalar.activation(qk_t[:, g].rearrange("p a t -> p (a t)"), misc[:, :],
                                     ACT.Copy).then_inc(stack_kept, 1)

            for g in range(GROUPS):
                keep_stack(g, g + 1)

            def sequence(b, last_one):
                for g in range(GROUPS):
                    n = 4 * b + g
                    for half in range(2):
                        act.wait_ge(s2_done[half], n + 1)
                        act.wait_ge(pv_done[half], after(n))
                        nc.scalar.activation(probs[half][:], s2[half][:, :, 0:SCORE_COLS],
                                             ACT.Exp).then_inc(exp_done[half], 1)
                    if g % 2:
                        grp = g // 2
                        act.wait_ge(pv_done[1], after(n + 1))
                        act.wait_ge(pv_turned[grp], after(b))
                        nc.scalar.activation(o_t[:, grp, :], pv[0:VROWS, grp * SEQ:(grp + 1) * SEQ],
                                             ACT.Copy).then_inc(pv_kept[grp], 1)
                    if not last_one:
                        keep_stack(g, n + GROUPS + 1)

            with act.Fori(0, LAST) as b:
                sequence(b, False)
            sequence(LAST, True)

            act.wait_ge(var2_ready, 1)
            nc.scalar.activation(std[:], veps[:], ACT.Sqrt).then_inc(std2_ready, 1)
            for c in range(CHUNKS):
                act.wait_ge(x_turned, c + 1)
                nc.scalar.activation(xh[:, c * CHUNK:(c + 1) * CHUNK], d_ps[c],
                                     ACT.Copy).then_inc(xh_ready, 1)
            act.wait_ge(shifted, 1)
            nc.scalar.activation(prob[:], logits[:], ACT.Exp).then_inc(gate_exp, 1)

            def silu_unit(k, pair):
                act.wait_ge(up_done, after(UNITS * pair + k + 1))
                act.wait_ge(mul_done[k % 2], after(UNITS // 2 * pair + k // 2))
                nc.scalar.activation(silu[k % 2][:], g_ps[k % 2], ACT.Silu)\
                    .then_inc(silu_done[k % 2], 1)

            def high_unit(k, pair):
                act.wait_ge(mul_done[k % 2], after(UNITS // 2 * pair + k // 2 + 1))
                act.wait_ge(down_done[k % 4], after(UNITS // 4 * pair + k // 4))
                nc.scalar.activation(hh[k % 4][:], hid[k % 2][:], ACT.Copy)\
                    .then_inc(hh_done[k % 4], 1)

            silu_unit(0, 0)
            act.wait_ge(comb_turned, 1)
            nc.scalar.activation(comb_t[:], misc[0:EXPERTS * TILES, 0:P], ACT.Copy)\
                .then_inc(comb_kept, 1)
            with act.Fori(0, PAIRS - 1) as pair:
                for k in range(UNITS):
                    silu_unit(k + 1, pair)
                    high_unit(k, pair)
            pair = PAIRS - 1
            for k in range(UNITS):
                if k + 1 < UNITS:
                    silu_unit(k + 1, pair)
                high_unit(k, pair)

        @block.gpsimd
        def _(pool):
            for s in (*hl_done, *summed):
                pool.sem_inc(s, 1)

            pool_steps = [0]

            def link(ins, base=0):
                pool_steps[0] += 1
                ins.then_inc(pool_chain, 1)
                pool.wait_ge(pool_chain, base + pool_steps[0])

            def none(n):
                return zeros[:, 0:n * HEAD_DIM].rearrange("p (n c) -> p n c", c=HEAD_DIM)

            def keys(b, base):
                pool.wait_ge(k_loaded, 16 * b + 16)
                src = k_in[:].rearrange("p n (h c) -> p (n h) c", c=HEAD_DIM)
                rows = k_nat[:, :, 0:QK_COLS].rearrange("p n (r c) -> p n r c", c=HEAD_DIM)
                nc.gpsimd.tensor_tensor(rows[:, :, 2, :].bitcast(F32R), src, none(TPB * HEADS),
                                        ALU.add)
                link(nc.gpsimd.tensor_tensor(rows[:, :, 0, :].bitcast(F32R), src,
                                             none(TPB * HEADS), ALU.add), base)
                nc.gpsimd.tensor_tensor(rows[:, :, 1, :].bitcast(F32R), src, rows[:, :, 0, :],
                                        ALU.subtract).then_inc(k_nat_ready, 1)

            def own_columns(t, grp):
                first = (t * HEADS + grp * HALF) * VROWS
                step = VROWS + VCOLS
                return v_pad[:, first:first + HALF * step]\
                    .rearrange("p (h c) -> p h c", c=step)[:, :, 0:VCOLS]

            def value_columns(b, grp):
                pool.wait_ge(v_loaded, 16 * b + 16)
                for t in range(TPB):
                    src = v_in[:, t, grp * HALF * HEAD_DIM:(grp + 1) * HALF * HEAD_DIM]
                    last = nc.gpsimd.tensor_tensor(own_columns(t, grp)[:, :, 0:HEAD_DIM],
                                                   src.rearrange("p (h c) -> p h c", c=HEAD_DIM),
                                                   none(HALF), ALU.add)
                last.then_inc(v_ready[grp], 1)

            link(nc.gpsimd.memset(zeros[:], 0.0))
            nc.gpsimd.memset(v_pad[:], 0.0).then_inc(pool_chain, 1)
            pool_steps[0] += 1
            pool.wait_ge(const_in, 16)
            nc.gpsimd.tensor_copy(k_nat[:, :, QK_COLS:ROWS], k_const)
            keys(0, 0)
            pool.wait_ge(pool_chain, 2)
            for t in range(TPB):
                for grp in range(2):
                    nc.gpsimd.memset(own_columns(t, grp)[:, :, HEAD_DIM:VCOLS], 1.0)
            for grp in range(2):
                value_columns(0, grp)
            nc.gpsimd.memset(acc[:], 0.0)
            before = pool_steps[0]
            with pool.Fori(0, LAST) as b:
                pool_steps[0] = before
                pool.wait_ge(stacked, 4 * b + GROUPS)
                keys(b + 1, b)
                for grp in range(2):
                    pool.wait_ge(pv_done[1], after(4 * b + 2 * grp + 2))
                    value_columns(b + 1, grp)

            def low_unit(k, pair):
                pool.wait_ge(hh_done[k % 4], UNITS // 4 * pair + k // 4 + 1)
                pool.wait_ge(down_done[k % 4], after(UNITS // 4 * pair + k // 4))
                nc.gpsimd.tensor_tensor(hl[k % 4][:], hid[k % 2][:], hh[k % 4][:].bitcast(F32),
                                        ALU.subtract).then_inc(hl_done[k % 4], 1)

            def add_chunk(c, count):
                pool.wait_ge(scaled[c], after(count))
                pool.wait_ge(summed[c], after(count - 1))
                nc.gpsimd.tensor_tensor(acc[:, c, :], acc[:, c, :], part[c][:], ALU.add)\
                    .then_inc(summed[c], 1)

            def experts(pair, last_one):
                for k in range(UNITS):
                    if not (last_one and k + LAG + 2 >= UNITS):
                        low_unit(k + LAG + 2, pair)
                    if k % FT == FT - 1:
                        add_chunk(k // FT % CHUNKS, 2 * pair + k // (FT * CHUNKS) + 1)

            for k in range(LAG + 2):
                low_unit(k, 0)
            with pool.Fori(0, PAIRS - 1) as pair:
                experts(pair, False)
            experts(PAIRS - 1, True)

        @block.vector
        def _(dve):
            for s in (*attn_done, *mul_done, *scaled):
                dve.sem_inc(s, 1)

            steps = [0]

            def link(ins, base=0):
                steps[0] += 1
                ins.then_inc(dve_chain, 1)
                dve.wait_ge(dve_chain, base + steps[0])

            nc.vector.memset(max_nat[:], 0.0)
            dve.wait_ge(const_in, 16)
            nc.vector.tensor_copy(cb[:].rearrange("p a n -> p (a n)"), cf[:, 0:3 * P])\
                .then_inc(masks_ready, 1)
            nc.vector.tensor_copy(q_nat[:, :, QK_COLS:ROWS], q_const)
            dve.wait_ge(first_in, 16)
            for t in range(TPB):
                nc.vector.bn_stats(bn[:, t, :], x_in[:, t, :])
            dve.wait_ge(rest_in, 16)
            for t in range(TPB, TILES):
                last = nc.vector.bn_stats(bn[:, t, :], x_in[:, t, :])
            link(last)
            for t in range(TILES):
                last = nc.vector.bn_aggr(stats[:, 2 * t:2 * t + 2], bn[:, t, :])
            link(last)
            var = stats[:].rearrange("p (t c) -> p t c", c=2)[:, :, 1]
            nc.vector.tensor_scalar_add(veps[:], var, EPS).then_inc(var_ready, 1)
            dve.wait_ge(std_ready, 1)
            link(nc.vector.reciprocal(rstd[:], std[:]))
            link(nc.vector.tensor_scalar(rstd_q[:], rstd[:], float(np.float32(1 / np.sqrt(8.0))),
                                         None, ALU.mult))

            def queries(b_next, base):
                for t in range(TPB):
                    at = TPB * b_next + t
                    last = nc.vector.tensor_scalar(
                        q_norm[:, t, :], x_in[:, ds(at, 1), :].rearrange("p a d -> p (a d)"),
                        stats[:, ds(2 * at, 1)], rstd_q[:, ds(at, 1)],
                        ALU.subtract, ALU.mult)
                link(last, base)
                src = q_norm[:].rearrange("p n (h c) -> p (n h) c", c=HEAD_DIM)
                rows = q_nat[:, :, 0:QK_COLS].rearrange("p n (r c) -> p n r c", c=HEAD_DIM)
                link(nc.vector.tensor_copy(
                    rows[:, :, 0:2, :].bitcast(F32R),
                    src.unsqueeze(2).broadcast_to([P, TPB * HEADS, 2, HEAD_DIM])), base)
                nc.vector.tensor_tensor(rows[:, :, 2, :].bitcast(F32R), src, rows[:, :, 0, :],
                                        ALU.subtract).then_inc(q_nat_ready, 1)

            def maxima(half, count):
                dve.wait_ge(s1_done[half], count)
                hs = slice(2 * half, 2 * half + 2)
                nc.vector.tensor_reduce(neg_max[:, 0, hs], s1[:, :, 0:P], AX.X, ALU.max,
                                        negate=True)
                return nc.vector.tensor_reduce(neg_max[:, 1, hs], s1[:, :, P:P + SEQ], AX.X,
                                               ALU.max, negate=True).then_inc(max_done[half], 1)

            def split_maxima(base, count):
                dve.wait_ge(max_turned, count - 1)
                dve.wait_ge(max_done[0], count)
                dve.wait_ge(max_done[1], count)
                link(nc.vector.tensor_copy(max_nat[:, :, :, MAX_COL].bitcast(F32R), neg_max[:]),
                     base)
                nc.vector.tensor_tensor(max_nat[:, :, :, MAX_COL + 1].bitcast(F32R), neg_max[:],
                                        max_nat[:, :, :, MAX_COL], ALU.subtract)\
                    .then_inc(max_split, 1)

            def place_maxima(g, count):
                dve.wait_ge(max_turned, count)
                dve.wait_ge(stack_kept, count)
                nc.vector.tensor_tensor(q_max_t[:, g, :], misc[:, 0:SEQ],
                                        qk_t[:, g, 0, :].bitcast(F32), ALU.add)\
                    .then_inc(q_max_ready, 1)

            def finish_heads(b, grp, base):
                dve.wait_ge(pv_turned[grp], after(b + 1))
                o = misc[:, 0:TPB * VROWS].rearrange("p (t h c) -> p t h c", t=TPB, c=VCOLS)
                link(nc.vector.reciprocal(r_den[:], o[:, :, :, HEAD_DIM]), base)
                nc.vector.tensor_tensor(
                    attn[:], o[:, :, :, 0:HEAD_DIM],
                    r_den[:].unsqueeze(3).broadcast_to([P, TPB, HALF, HEAD_DIM]), ALU.mult)\
                    .then_inc(attn_done[grp], 1)
                dve.wait_ge(attn_done[grp], after(b + 1))
                cols = slice(grp * HALF * HEAD_DIM, (grp + 1) * HALF * HEAD_DIM)
                return nc.vector.tensor_tensor(
                    x_mid[:, ds(TPB * b, TPB), cols], attn[:].rearrange("p t h c -> p t (h c)"),
                    x_in[:, ds(TPB * b, TPB), cols], ALU.add)

            queries(0, 0)
            maxima(0, 1)
            maxima(1, 1)
            split_maxima(0, 1)
            place_maxima(0, 1)

            def sequence(b, last_one, per):
                base = per * b
                if not last_one:
                    dve.wait_ge(stacked, 4 * b + GROUPS)
                    queries(b + 1, base)
                for g in range(GROUPS):
                    n = 4 * b + g
                    if not (last_one and g == GROUPS - 1):
                        maxima(0, n + 2)
                        maxima(1, n + 2)
                        split_maxima(base, n + 2)
                        place_maxima((g + 1) % GROUPS, n + 2)
                    if g >= 2:
                        last = finish_heads(b, g - 2, base)
                    if last_one and g == 0:
                        moments(range(TPB * LAST), base)
                return last

            def moments(tiles, base):
                for t in tiles:
                    last = nc.vector.bn_stats(bn[:, t, :], x_mid[:, t, :])
                link(last, base)
                for t in tiles:
                    last = nc.vector.bn_aggr(stats[:, 2 * t:2 * t + 2], bn[:, t, :])
                return last

            before = steps[0]
            PER = 8
            with dve.Fori(0, LAST) as b:
                steps[0] = before
                sequence(b, False, PER)
            assert steps[0] - before == PER, steps[0] - before
            steps[0] = before
            base = PER * LAST
            link(sequence(LAST, True, PER), base)
            link(moments(range(TPB * LAST, TILES), base), base)

            nc.vector.tensor_scalar_add(veps[:], var, EPS).then_inc(var2_ready, 1)
            dve.wait_ge(std2_ready, 1)
            link(nc.vector.reciprocal(rstd[:], std[:]), base)
            for t in range(TILES):
                last = nc.vector.tensor_scalar(x_norm[:, t, :], x_mid[:, t, :],
                                               stats[:, 2 * t:2 * t + 1], rstd[:, t:t + 1],
                                               ALU.subtract, ALU.mult)
                if t % (TILES // 2) == TILES // 2 - 1:
                    last.then_inc(x_norm_ready, 1)
            dve.wait_ge(gate_in, 32)
            link(nc.vector.tensor_copy(gate_hl[:, 0, :], gate_sb[:]), base)
            nc.vector.tensor_tensor(gate_hl[:, 1, :], gate_sb[:], gate_hl[:, 0, :].bitcast(F32),
                                    ALU.subtract).then_inc(gate_ready, 1)
            for c in range(CHUNKS):
                xs = slice(c * CHUNK, (c + 1) * CHUNK)
                dve.wait_ge(xh_ready, c + 1)
                nc.vector.tensor_tensor(xl[:, xs], d_ps[c], xh[:, xs].bitcast(F32),
                                        ALU.subtract).then_inc(xl_ready, 1)

            w_sb = (w1_sb, w3_sb, w2_sb)

            def split_weights(i, m, e, count):
                src = w_sb[m][:, ds(e * FFN, FFN)]
                ins = nc.vector.tensor_copy(wh[i][m][:], src)
                ins.then_inc(w_high, 1)
                dve.wait_ge(w_high, count)
                nc.vector.tensor_tensor(wl[i][m][:], src, wh[i][m][:].bitcast(F32),
                                        ALU.subtract).then_inc(w_split[i], 1)

            dve.wait_ge(w_in, 48)
            for m in range(3):
                split_weights(0, m, 0, m + 1)

            dve.wait_ge(logits_done, 1)
            link(nc.vector.tensor_tensor(
                logits[:], pv[:, 0:TILES * EXPERTS].rearrange("p (t e) -> p t e", e=EXPERTS),
                bias_sb[:].unsqueeze(1).broadcast_to([P, TILES, EXPERTS]), ALU.add), base)
            link(nc.vector.tensor_reduce(row[:], logits[:], AX.X, ALU.max), base)
            nc.vector.tensor_tensor(logits[:], logits[:],
                                    row[:].unsqueeze(2).broadcast_to([P, TILES, EXPERTS]),
                                    ALU.subtract).then_inc(shifted, 1)
            dve.wait_ge(gate_exp, 1)
            link(nc.vector.tensor_reduce(row[:], prob[:], AX.X, ALU.add), base)
            link(nc.vector.reciprocal(row[:], row[:]), base)
            link(nc.vector.tensor_tensor(prob[:], prob[:],
                                         row[:].unsqueeze(2).broadcast_to([P, TILES, EXPERTS]),
                                         ALU.mult), base)
            for t in range(TILES):
                last = nc.vector.max(top[:, t, :], prob[:, t, :])
            link(last, base)
            link(nc.vector.tensor_tensor(row[:], top[:, :, 0], top[:, :, 1], ALU.add), base)
            link(nc.vector.memset(top[:, :, TOP_K:], -1.0), base)
            for t in range(TILES):
                nc.vector.match_replace(rest[:, t, :], top[:, t, :], prob[:, t, :], 0.0)
            link(nc.vector.reciprocal(row[:], row[:]), base)
            link(nc.vector.tensor_tensor(prob[:], prob[:], rest[:], ALU.subtract), base)
            nc.vector.tensor_tensor(comb[:].rearrange("p e t -> p t e"), prob[:],
                                    row[:].unsqueeze(2).broadcast_to([P, TILES, EXPERTS]),
                                    ALU.mult).then_inc(comb_ready, 1)

            def multiply(k, pair):
                dve.wait_ge(silu_done[k % 2], after(UNITS // 2 * pair + k // 2 + 1))
                dve.wait_ge(hl_done[(k - 2) % 4], after(UNITS // 4 * pair + (k - 2) // 4 + 1))
                nc.vector.tensor_tensor(hid[k % 2][:], silu[k % 2][:], u_ps[k % 2], ALU.mult)\
                    .then_inc(mul_done[k % 2], 1)

            def scale(k, pair):
                i, c = k // (CHUNKS * FT), k // FT % CHUNKS
                dve.wait_ge(down_done[k % 4], after(UNITS // 4 * pair + k // 4 + 1))
                dve.wait_ge(comb_in[i], 16 * (pair + 1))
                dve.wait_ge(summed[c], after(2 * pair + i))
                nc.vector.tensor_tensor(part[c][:], d_ps[c],
                                        comb_all[i][:, c * CHUNK:(c + 1) * CHUNK], ALU.mult)\
                    .then_inc(scaled[c], 1)

            def experts(pair, last_one):
                count = 3 + 6 * pair
                for k in range(UNITS):
                    if k < 2:
                        dve.wait_ge(up_done, after(UNITS * pair))
                        split_weights(1, k, 2 * pair + 1, count + k + 1)
                    if k == 2:
                        dve.wait_ge(down_done[3], after(UNITS // 4 * pair))
                        split_weights(1, k, 2 * pair + 1, count + k + 1)
                    if not last_one and k in (6, 7):
                        dve.wait_ge(up_done, after(UNITS * pair + UNITS // 2))
                        split_weights(0, k - 6, 2 * pair + 2, count + k - 6 + 4)
                    if not last_one and k == 8:
                        dve.wait_ge(down_done[3], after(UNITS // 4 * pair + UNITS // 8))
                        split_weights(0, k - 6, 2 * pair + 2, count + k - 6 + 4)
                    if not (last_one and k + LAG + 1 >= UNITS):
                        multiply(k + LAG + 1, pair)
                    if k % FT == FT - 1:
                        scale(k, pair)

            for k in range(LAG + 1):
                multiply(k, 0)
            with dve.Fori(0, PAIRS - 1) as pair:
                experts(pair, False)
            experts(PAIRS - 1, True)

            half = TILES // 2
            for c in range(CHUNKS):
                dve.wait_ge(y_turned, c + 1)
                nc.vector.tensor_tensor(
                    y[:, c * half:(c + 1) * half, :].rearrange("p t d -> p (t d)"),
                    banks[:, 6 + c, :],
                    x_mid[:, c * half:(c + 1) * half, :].rearrange("p t d -> p (t d)"),
                    ALU.add).then_inc(y_ready, 1)


_INS = ["x", "ctx_1024", "L0_ffn_gate_w", "L0_ffn_gate_b", "L0_ffn_w1", "L0_ffn_w3", "L0_ffn_w2"]


def kernel(**inputs):
    import concourse.bacc as bacc
    from concourse.bass_utils import run_bass_kernel_spmd

    nc = bacc.Bacc("TRN2", target_bir_lowering=False, num_devices=1)
    arrays = {name: np.ascontiguousarray(inputs[name]) for name in _INS}
    for name in ("x", "ctx_1024", "L0_ffn_w2"):
        arrays[name] = arrays[name].reshape(-1, D)
    arrays["consts"] = constants()
    arrays = {f"in_{name}": a for name, a in arrays.items()}
    args = [nc.dram_tensor(name, a.shape, mybir.dt.from_np(a.dtype), kind="ExternalInput").ap()
            for name, a in arrays.items()]
    out = nc.dram_tensor("out", (TOKENS, D), mybir.dt.float32, kind="ExternalOutput").ap()
    c_dram = nc.dram_tensor("c_dram", (EXPERTS * TILES, P), mybir.dt.float32, kind="Internal").ap()
    build(nc, *args, out, c_dram)
    r = run_bass_kernel_spmd(nc, [arrays], core_ids=[0])
    return r.results[0]["out"].reshape(BATCH, SEQ, D)
```

```python
from contextlib import ExitStack

import numpy as np
import concourse.bass as bass
from concourse import mybir

P = 128
BATCH, SEQ, D = 4, 256, 128
HEADS, HEAD_DIM = 16, 8
EXPERTS, FFN, TOP_K = 8, 512, 2
EPS = 1e-5

TILES = BATCH * SEQ // P
TPB = SEQ // P
GROUPS = HEADS // 4
ROWS = 32
QK_COLS = 3 * HEAD_DIM
MAX_COL = QK_COLS + 4
VCOLS = HEAD_DIM + 1
VHIGH = 4 * VCOLS
VROWS = 2 * VHIGH
HALF = HEADS // 2
SCORE_COLS = SEQ + P
FT = FFN // P
TOKENS = BATCH * SEQ
CHUNK = 512
CHUNKS = TOKENS // CHUNK
UNITS = 2 * CHUNKS * FT
LAG = 3


def constants():
    def high(a):
        bits = np.ascontiguousarray(a, np.float32).view(np.uint32).astype(np.uint64)
        return ((bits + 0x800) & 0xFFFFF000).astype(np.uint32).view(np.float32)

    slope = np.cumprod(np.full(HEADS, 2.0 ** (-8.0 / HEADS), np.float32), dtype=np.float32)
    token = np.arange(SEQ, dtype=np.float32).reshape(TPB, P).T[:, :, None]
    q = np.zeros((P, TPB, HEADS, 8), np.float32)
    k = np.zeros((P, TPB, HEADS, 8), np.float32)
    down = (-token * slope).astype(np.float32)
    q[..., 0], q[..., 1] = high(slope), slope - high(slope)
    q[..., 2], q[..., 3] = high(down), down - high(down)
    k[..., 0] = k[..., 1] = token
    k[..., 2:6] = 1.0
    p = np.arange(P)
    fold = (p[:, None] % VHIGH == np.arange(VHIGH)) & (p[:, None] < VROWS)
    return np.concatenate([np.eye(P), np.where(p[None, :] > p[:, None], -1e30, 0.0),
                           np.where(p[:, None] > p[None, :], -1e30, 0.0),
                           q.reshape(P, -1), k.reshape(P, -1), fold], 1).astype(np.float32)


def build(nc, x, ctx_in, gate_w, gate_b, w1, w3, w2, consts, out, c_dram):
    F32, F32R, BF16 = mybir.dt.float32, mybir.dt.float32r, mybir.dt.bfloat16
    ALU, ACT, AX = mybir.AluOpType, mybir.ActivationFunctionType, mybir.AxisListType
    ds = bass.ds

    with ExitStack() as stack:
        def sb(name, shape, dt=F32):
            return stack.enter_context(nc.sbuf_tensor(name, shape, dt))

        def sem(name):
            return stack.enter_context(nc.semaphore(name))

        n_const = TPB * HEADS * 8
        cf = sb("cf", [P, 3 * P + 2 * n_const + VHIGH])
        ident = cf[:, 0:P]
        q_const = cf[:, 3 * P:3 * P + n_const].rearrange("p (n c) -> p n c", c=8)
        k_const = cf[:, 3 * P + n_const:3 * P + 2 * n_const].rearrange("p (n c) -> p n c", c=8)
        fold = cf[0:VROWS, 3 * P + 2 * n_const:]
        cb = sb("cb", [P, 3, P], BF16)
        x_in = sb("x_in", [P, TILES, D])
        k_in = sb("k_in", [P, TPB, D])
        v_in = sb("v_in", [P, TPB, D])
        gate_sb = sb("gate_sb", [P, EXPERTS])
        bias_sb = sb("bias_sb", [P, EXPERTS])
        w1_sb = sb("w1_sb", [P, EXPERTS * FFN])
        w3_sb = sb("w3_sb", [P, EXPERTS * FFN])
        w2_sb = sb("w2_sb", [P, EXPERTS * FFN])
        bn = sb("bn", [P, TILES, 6])
        stats = sb("stats", [P, TILES * 2])
        veps = sb("veps", [P, TILES])
        power = sb("power", [P, TILES])
        rstd = sb("rstd", [P, TILES])
        q_norm = sb("q_norm", [P, TPB, D])
        q_nat = sb("q_nat", [P, TPB * HEADS, ROWS])
        k_nat = sb("k_nat", [P, TPB * HEADS, ROWS])
        qk_t = sb("qk_t", [P, GROUPS, 2, SEQ], F32R)
        q_max_t = sb("q_max_t", [P, GROUPS, SEQ], F32R)
        neg_max = sb("neg_max", [P, TPB, 4])
        max_nat = sb("max_nat", [P, TPB, 4, ROWS])
        zeros = sb("zeros", [P, TPB * D])
        v_pad = sb("v_pad", [P, TPB * HEADS * VROWS + VROWS], F32R)
        probs = [sb(f"probs{i}", [P, 2, SCORE_COLS]) for i in range(2)]
        p_high = [[sb(f"p_high{i}{h}", [P, 2, SCORE_COLS], F32R) for h in range(2)]
                  for i in range(2)]
        p_low = [[sb(f"p_low{i}{h}", [P, 2, SCORE_COLS], F32R) for h in range(2)]
                 for i in range(2)]
        o_t = sb("o_t", [VROWS, GROUPS, SEQ])
        r_den = sb("r_den", [P, TPB, HALF])
        attn = sb("attn", [P, TPB, HALF, HEAD_DIM])
        x_mid = sb("x_mid", [P, TILES, D])
        x_norm = sb("x_norm", [P, TILES, D])
        xh = sb("xh", [P, TOKENS], F32R)
        xl = sb("xl", [P, TOKENS], F32R)
        gate_hl = sb("gate_hl", [P, 2, EXPERTS], F32R)
        logits = sb("logits", [P, TILES, EXPERTS])
        row = sb("row", [P, TILES])
        prob = sb("prob", [P, TILES, EXPERTS])
        top = sb("top", [P, TILES, 8])
        rest = sb("rest", [P, TILES, EXPERTS])
        comb = sb("comb", [P, EXPERTS, TILES])
        comb_t = sb("comb_t", [P, EXPERTS * TILES])
        comb_all = [sb(f"comb_all{i}", [P, TOKENS]) for i in range(2)]
        wh = [[sb(f"wh{m}_{i}", [P, FFN], F32R) for m in range(3)] for i in range(2)]
        wl = [[sb(f"wl{m}_{i}", [P, FFN], F32R) for m in range(3)] for i in range(2)]
        silu = [sb(f"silu{i}", [P, CHUNK]) for i in range(2)]
        hid = [sb(f"hid{i}", [P, CHUNK]) for i in range(2)]
        hh = [sb(f"hh{i}", [P, CHUNK], F32R) for i in range(4)]
        hl = [sb(f"hl{i}", [P, CHUNK], F32R) for i in range(4)]
        part = [sb(f"part{i}", [P, CHUNK]) for i in range(2)]
        acc = sb("acc", [P, CHUNKS, CHUNK])
        y = x_norm

        banks = stack.enter_context(nc.psum_tensor("banks", [P, 8, 512], F32))
        s1 = banks[:, 0:2]
        s2 = [banks[:, 2:4], banks[:, 4:6]]
        pv = banks[:, 6]
        misc = banks[:, 7]
        g_ps = [banks[:, 0], banks[:, 1]]
        u_ps = [banks[:, 2], banks[:, 3]]
        d_ps = [banks[:, 4], banks[:, 5]]

        k_rows = k_nat[:, :, 0:QK_COLS].rearrange("p n (r c) -> p n r c", c=HEAD_DIM)
        w_sb = (w1_sb, w3_sb, w2_sb)

        first_s1 = ((s1, banks[:, 5:7]), (banks[:, 2:4], s1), (banks[:, 5:7], s1))
        by_scores = s1[:, :, SCORE_COLS:SCORE_COLS + VROWS]
        in_misc = misc[:, 0:TPB * VROWS].rearrange("p (t c) -> p t c", t=TPB)

        def diagonal(bank):
            return bank.rearrange("p (a b) -> p a b", b=SEQ)[:, :, 0:P]

        const_in = sem("const_in")
        first_in = sem("first_in")
        k_loaded = sem("k_loaded")
        v_loaded = sem("v_loaded")
        rest_in = sem("rest_in")
        gate_in = sem("gate_in")
        w_in = sem("w_in")
        comb_out = sem("comb_out")
        comb_in = [sem(f"comb_in{i}") for i in range(2)]
        out_sem = sem("out_sem")
        dve_chain = sem("dve_chain")
        pool_chain = sem("pool_chain")
        masks_ready = sem("masks_ready")
        var_ready = sem("var_ready")
        power_ready = sem("power_ready")
        rstd_ready = sem("rstd_ready")
        q_nat_ready = sem("q_nat_ready")
        k_nat_ready = sem("k_nat_ready")
        v_ready = [sem(f"v_ready{i}") for i in range(2)]
        stacked = sem("stacked")
        stack_kept = sem("stack_kept")
        s1_done = [sem(f"s1_done{i}") for i in range(2)]
        max_done = [sem(f"max_done{i}") for i in range(2)]
        max_split = sem("max_split")
        max_turned = sem("max_turned")
        q_max_ready = sem("q_max_ready")
        s2_done = [sem(f"s2_done{i}") for i in range(2)]
        exp_done = [sem(f"exp_done{i}") for i in range(2)]
        low_done = [sem(f"low_done{i}") for i in range(2)]
        pv_done = [sem(f"pv_done{i}") for i in range(2)]
        pv_kept = sem("pv_kept")
        pv_turned = [sem(f"pv_turned{i}") for i in range(2)]
        attn_done = [sem(f"attn_done{i}") for i in range(2)]
        x_norm_ready = sem("x_norm_ready")
        x_turned = sem("x_turned")
        xh_ready = sem("xh_ready")
        xl_ready = sem("xl_ready")
        gate_ready = sem("gate_ready")
        logits_done = sem("logits_done")
        shifted = sem("shifted")
        gate_exp = sem("gate_exp")
        logits_kept = sem("logits_kept")
        comb_turned = sem("comb_turned")
        k_high = sem("k_high")
        w_first_high = sem("w_first_high")
        w_first = sem("w_first")
        w_high = sem("w_high")
        w_split = [sem(f"w_split{i}") for i in range(2)]
        up_done = sem("up_done")
        silu_done = [sem(f"silu_done{i}") for i in range(2)]
        mul_done = [sem(f"mul_done{i}") for i in range(2)]
        hh_done = [sem(f"hh_done{i}") for i in range(4)]
        hl_done = [sem(f"hl_done{i}") for i in range(4)]
        down_done = [sem(f"down_done{i}") for i in range(4)]
        scaled = [sem(f"scaled{i}") for i in range(2)]
        summed = [sem(f"summed{i}") for i in range(2)]
        y_turned = sem("y_turned")
        y_ready = sem("y_ready")

        def after(n):
            return n + 1

        block = stack.enter_context(nc.Block())

        X_PIECES = ((0, 4), (4, 6), (6, 8))
        LAST = BATCH - 1
        PAIRS = EXPERTS // 2

        @block.sync
        def _(sp):
            tiled = lambda a: a.rearrange("(n p) d -> p n d", p=P)
            sp.dma_start(x_in[:, 0:TPB], tiled(x)[:, 0:TPB]).then_inc(first_in, 16)
            sp.dma_start(k_in[:], tiled(ctx_in)[:, 0:TPB]).then_inc(k_loaded, 16)
            sp.dma_start(v_in[:], tiled(ctx_in)[:, 0:TPB]).then_inc(v_loaded, 16)
            sp.dma_start(x_in[:, TPB:], tiled(x)[:, TPB:]).then_inc(rest_in, 16)
            sp.dma_start(gate_sb[:], gate_w).then_inc(gate_in, 16)
            sp.dma_start(bias_sb[:], gate_b.partition_broadcast(P)).then_inc(gate_in, 16)
            for w_sb_, w in ((w1_sb, w1), (w3_sb, w3)):
                sp.dma_start(w_sb_[:].rearrange("p (e f) -> p e f", e=EXPERTS),
                             w.rearrange("e d f -> d e f")).then_inc(w_in, 16)
            sp.dma_start(w2_sb[:].rearrange("p (n d) -> p n d", d=D),
                         w2.rearrange("(n p) d -> p n d", p=P)).then_inc(w_in, 16)
            with sp.Fori(1, BATCH) as b:
                sp.wait_ge(k_nat_ready, b)
                sp.dma_start(k_in[:], tiled(ctx_in)[:, ds(TPB * b, TPB)]).then_inc(k_loaded, 16)
                sp.wait_ge(v_ready[0], b)
                sp.wait_ge(v_ready[1], b)
                sp.dma_start(v_in[:], tiled(ctx_in)[:, ds(TPB * b, TPB)]).then_inc(v_loaded, 16)
            sp.wait_ge(comb_turned, 1)
            for q in range(P // 32):
                sp.dma_start(c_dram[:, 32 * q:32 * q + 32].rearrange("(c i) j -> i c j", i=32),
                             comb_t[32 * q:32 * q + 32, :].rearrange("i (c j) -> i c j", j=32))\
                    .then_inc(comb_out, 16)
            sp.wait_ge(comb_out, 16 * (P // 32))
            rows = c_dram.rearrange("(e n) t -> e (n t)", e=EXPERTS)
            def load_comb(i, e):
                sp.dma_start(comb_all[i][:], rows[ds(e, 1), :].rearrange("a t -> (a t)")
                             .partition_broadcast(P)).then_inc(comb_in[i], 16)

            for i in range(2):
                load_comb(i, i)
            with sp.Fori(1, PAIRS) as pair:
                for i in range(2):
                    for c in range(CHUNKS):
                        sp.wait_ge(scaled[c], after(2 * pair + (i - 1)))
                    load_comb(i, 2 * pair + i)
            flat = tiled(out)
            half = TILES // 2
            for c in range(2):
                sp.wait_ge(y_ready, c + 1)
                sp.dma_start(flat[:, c * half:(c + 1) * half],
                             y[:, c * half:(c + 1) * half]).then_inc(out_sem, 16)
            sp.wait_ge(out_sem, 32)

        @block.tensor
        def _(pe):
            for s in (*pv_done, *pv_turned, up_done, *down_done):
                pe.sem_inc(s, 1)

            def stack_group(g, bank):
                for nat, at in ((q_nat, 0), (k_nat, SEQ)):
                    for t in range(TPB):
                        src = nat[:, t * HEADS + 4 * g:t * HEADS + 4 * g + 4, :]
                        last = nc.tensor.transpose(bank[:, at + t * P:at + (t + 1) * P],
                                                   src.rearrange("p h r -> p (h r)"), ident)
                last.then_inc(stacked, 1)

            def masked(banks_, mask):
                for j in range(2):
                    nc.tensor.matmul(diagonal(banks_[:, j]), cb[:, 0, :],
                                     mask.unsqueeze(1).broadcast_to([P, 2, P]),
                                     start=True, stop=False, skip_group_check=True)

            def rows_of(half, j):
                return slice(ROWS * (2 * half + j), ROWS * (2 * half + j + 1))

            def scores_for_maxima(g, half, s1=s1):
                masked(s1, cb[:, 1, :])
                for j in range(2):
                    q, k = qk_t[rows_of(half, j), g, 0, :], qk_t[rows_of(half, j), g, 1, :]
                    nc.tensor.matmul(s1[:, j, P:P + SEQ], q[:, P:SEQ], k[:, 0:SEQ],
                                     start=False, stop=False, skip_group_check=True)
                for j in range(2):
                    q, k = qk_t[rows_of(half, j), g, 0, :], qk_t[rows_of(half, j), g, 1, :]
                    last = nc.tensor.matmul(s1[:, j, 0:P], q[:, 0:P], k[:, 0:P],
                                            start=False, stop=True, skip_group_check=True)
                last.then_inc(s1_done[half], 1)

            def scores_for_exp(g, half):
                masked(s2[half], cb[:, 2, :])
                for j in range(2):
                    q, k = q_max_t[rows_of(half, j), g, :], qk_t[rows_of(half, j), g, 1, :]
                    nc.tensor.matmul(s2[half][:, j, 0:SEQ], k[:, 0:P], q[:, 0:SEQ],
                                     start=False, stop=False, skip_group_check=True)
                for j in range(2):
                    q, k = q_max_t[rows_of(half, j), g, :], qk_t[rows_of(half, j), g, 1, :]
                    last = nc.tensor.matmul(s2[half][:, j, SEQ:SEQ + P], k[:, P:SEQ], q[:, P:SEQ],
                                            start=False, stop=True, skip_group_check=True)
                last.then_inc(s2_done[half], 1)

            def values(g, half):
                sums = pv[0:VROWS, 0:SEQ]
                for j in range(2):
                    h = 4 * g + 2 * half + j
                    first, final = 2 * half + j == 0, 2 * half + j == 3
                    for t, cols, to in ((0, slice(0, SEQ), sums),
                                        (1, slice(SEQ, SEQ + P), sums[:, P:SEQ])):
                        own = v_pad[:, (t * HEADS + h) * VROWS:(t * HEADS + h + 1) * VROWS]
                        nc.tensor.matmul(to, own, p_high[g % 2][half][:, j, cols],
                                         start=first and t == 0, stop=False,
                                         skip_group_check=True)
                        last = nc.tensor.matmul(to, own, p_low[g % 2][half][:, j, cols],
                                                start=False, stop=final and t == 1,
                                                skip_group_check=True)
                last.then_inc(pv_done[half], 1)

            def turn_max():
                for t in range(TPB):
                    last = nc.tensor.transpose(misc[:, t * P:(t + 1) * P],
                                               max_nat[:, t].rearrange("p h r -> p (h r)"), ident)
                last.then_inc(max_turned, 1)

            def turn_values(grp, to):
                for t in range(TPB):
                    for i in range(2):
                        last = nc.tensor.matmul(to[:, t, i * VHIGH:(i + 1) * VHIGH],
                                                o_t[:, 2 * grp + i, t * P:(t + 1) * P], fold,
                                                start=True, stop=True)
                last.then_inc(pv_turned[grp], 1)

            def turn_x(tiles):
                for i, t in enumerate(tiles):
                    last = nc.tensor.transpose(misc[:, i * P:(i + 1) * P], x_norm[:, t, :], ident)
                last.then_inc(x_turned, 1)

            pe.wait_ge(const_in, 16)
            pe.wait_ge(q_nat_ready, 1)
            pe.wait_ge(k_nat_ready, 1)
            stack_group(0, misc)
            stack_group(1, banks[:, 2])
            pe.wait_ge(masks_ready, 1)
            pe.wait_ge(stack_kept, 1)
            scores_for_maxima(0, 0)
            stack_group(2, banks[:, 3])
            stack_group(3, banks[:, 4])
            scores_for_maxima(0, 1, first_s1[0][1])
            pe.wait_ge(stack_kept, 3)
            scores_for_maxima(1, 0, first_s1[1][0])
            pe.wait_ge(max_done[0], 1)
            scores_for_maxima(1, 1, first_s1[1][1])
            pe.wait_ge(max_split, 1)
            turn_max()
            pe.wait_ge(max_done[1], 1)
            scores_for_maxima(2, 0, first_s1[2][0])
            pe.wait_ge(max_done[0], 2)
            pe.wait_ge(q_max_ready, 1)
            scores_for_exp(0, 0)
            pe.wait_ge(max_done[1], 2)
            scores_for_maxima(2, 1, first_s1[2][1])
            pe.wait_ge(max_split, 2)
            turn_max()
            pe.wait_ge(max_done[0], 3)
            pe.wait_ge(stack_kept, GROUPS)
            scores_for_exp(0, 1)

            def sequence(b, last_one):
                for g in range(GROUPS):
                    n = 4 * b + g
                    more = [not last_one or g + ahead < GROUPS for ahead in range(4)]
                    if more[1]:
                        pe.wait_ge(q_max_ready, n + 2)
                        pe.wait_ge(exp_done[0], after(n + 1))
                        scores_for_exp((g + 1) % GROUPS, 0)
                    if more[3]:
                        pe.wait_ge(max_done[1], n + 3)
                        if g == 0:
                            pe.wait_ge(attn_done[1], after(b))
                        pe.wait_ge(stack_kept, n + 4)
                        scores_for_maxima((g + 3) % GROUPS, 0)
                    pe.wait_ge(pv_kept, after(n))
                    if not last_one and g == 2:
                        turn_values(0, by_scores)
                    if last_one and g == 2:
                        pe.wait_ge(xl_ready, 1)
                        turn_values(0, in_misc)
                    if last_one and g == 3:
                        pe.wait_ge(exp_done[0], after(n + 1))
                        pe.wait_ge(w_first, 2)
                        up(0, 0, 0)
                    if g % 2 == 0:
                        pe.wait_ge(v_ready[g // 2], b + 1)
                    pe.wait_ge(low_done[0], n + 1)
                    values(g, 0)
                    if more[2]:
                        pe.wait_ge(max_split, n + 3)
                        pe.wait_ge(stack_kept, GROUPS * BATCH if last_one else n + 4)
                        turn_max()
                    if more[1]:
                        pe.wait_ge(exp_done[1], after(n + 1))
                        scores_for_exp((g + 1) % GROUPS, 1)
                    pe.wait_ge(low_done[1], n + 1)
                    values(g, 1)
                    if more[3]:
                        pe.wait_ge(max_done[0], n + 4)
                        if g == 2:
                            pe.wait_ge(attn_done[0], after(b + 1))
                        scores_for_maxima((g + 3) % GROUPS, 1)
                        if g == GROUPS - 1:
                            pe.wait_ge(pv_kept, after(n + 1))
                            turn_values(1, by_scores)
                    if not last_one:
                        if g == 0:
                            pe.wait_ge(q_nat_ready, b + 2)
                            pe.wait_ge(k_nat_ready, b + 2)
                        pe.wait_ge(q_max_ready, n + 3)
                        stack_group(g, misc)
                    if last_one and g == 1:
                        pe.wait_ge(q_max_ready, n + 3)
                        pe.wait_ge(x_norm_ready, 1)
                        turn_x(range(4))
                    if last_one and g == 2:
                        pe.wait_ge(attn_done[0], after(b + 1))
                        pe.wait_ge(x_norm_ready, 2)
                        turn_x(range(4, 6))
                    if last_one and g == 3:
                        up(1, 0, 0)
                        pe.wait_ge(xl_ready, 2)
                        pe.wait_ge(pv_kept, after(n + 1))
                        turn_values(1, in_misc)

            def gate(tiles):
                for t in tiles:
                    o = misc[:, SEQ + t * EXPERTS:SEQ + (t + 1) * EXPERTS]
                    at = slice(t * P, (t + 1) * P)
                    nc.tensor.matmul(o, xh[:, at], gate_hl[:, 0, :], start=True, stop=False)
                    nc.tensor.matmul(o, xh[:, at], gate_hl[:, 1, :], start=False, stop=False)
                    last = nc.tensor.matmul(o, xl[:, at], gate_hl[:, 0, :], start=False, stop=True)
                return last

            def up(k, base, pair):
                i, c, j = k // (CHUNKS * FT) % 2, k // FT % CHUNKS, k % FT
                n = k % UNITS
                turn = base + k // 2
                if c == 0 and j == 0 and k:
                    pe.wait_ge(w_split[i], after(3 * (pair + k // UNITS - 1 + i) + 1))
                xs = slice(c * CHUNK, (c + 1) * CHUNK)
                js = slice(j * P, (j + 1) * P)
                for m, ps in ((0, g_ps[n % 2]), (1, u_ps[n % 2])):
                    if m == 0:
                        pe.wait_ge(silu_done[n % 2], after(turn))
                    else:
                        if c == 0 and j == 0 and k:
                            pe.wait_ge(w_split[i], after(3 * (pair + k // UNITS - 1 + i) + 2))
                        pe.wait_ge(mul_done[n % 2], after(turn))
                    nc.tensor.matmul(ps, wh[i][m][:, js], xh[:, xs], start=True, stop=False)
                    nc.tensor.matmul(ps, wh[i][m][:, js], xl[:, xs], start=False, stop=False)
                    last = nc.tensor.matmul(ps, wl[i][m][:, js], xh[:, xs], start=False, stop=True)
                last.then_inc(up_done, 1)

            def down(k, pair):
                i, c, j = k // (CHUNKS * FT), k // FT % CHUNKS, k % FT
                if j == 0:
                    pe.wait_ge(scaled[c], after(2 * pair + i))
                    if c == 0:
                        pe.wait_ge(w_split[i], after(3 * (pair + i)))
                pe.wait_ge(hl_done[k % 4], after(UNITS // 4 * pair + k // 4 + 1))
                js = slice(j * P, (j + 1) * P)
                h, l = hh[k % 4][:], hl[k % 4][:]
                nc.tensor.matmul(d_ps[c], wh[i][2][:, js], h, start=j == 0, stop=False)
                nc.tensor.matmul(d_ps[c], wh[i][2][:, js], l, start=False, stop=False)
                nc.tensor.matmul(d_ps[c], wl[i][2][:, js], h, start=False,
                                 stop=j == FT - 1).then_inc(down_done[k % 4], 1)

            with pe.Fori(0, LAST) as b:
                sequence(b, False)
            sequence(LAST, True)

            up(2, 0, 0)
            pe.wait_ge(attn_done[1], after(BATCH))
            pe.wait_ge(gate_ready, 1)
            gate(range(6))
            pe.wait_ge(x_norm_ready, 3)
            turn_x(range(6, 8))
            pe.wait_ge(xl_ready, 3)
            gate(range(6, 8)).then_inc(logits_done, 1)
            pe.wait_ge(w_first, 3)
            with pe.Fori(0, PAIRS - 1) as pair:
                for k in range(UNITS):
                    up(k + LAG, UNITS // 2 * pair, pair)
                    down(k, pair)
            pair = PAIRS - 1
            for k in range(UNITS):
                if k + LAG < UNITS:
                    up(k + LAG, UNITS // 2 * pair, pair)
                down(k, pair)
            for c in range(CHUNKS):
                pe.wait_ge(summed[c], after(EXPERTS))
                for t in range(CHUNK // P):
                    last = nc.tensor.transpose(banks[:, 6 + c, t * P:(t + 1) * P],
                                               acc[:, c, t * P:(t + 1) * P], ident)
                last.then_inc(y_turned, 1)

        @block.scalar
        def _(act):
            for s in (*exp_done, pv_kept, *silu_done):
                act.sem_inc(s, 1)

            act.dma_start(cf[:], consts).then_inc(const_in, 16)
            act.wait_ge(k_loaded, 16)
            k_src = k_in[:].rearrange("p n (h c) -> p (n h) c", c=HEAD_DIM)
            nc.scalar.activation(k_rows[:, :, 2, :].bitcast(F32R), k_src, ACT.Copy)
            nc.scalar.activation(k_rows[:, :, 0, :].bitcast(F32R), k_src, ACT.Copy)
            act.wait_ge(const_in, 16)
            nc.scalar.activation(k_nat[:, :, QK_COLS:ROWS], k_const, ACT.Copy)\
                .then_inc(k_high, 1)

            def keep_stack(g, bank, count):
                act.wait_ge(stacked, count)
                nc.scalar.activation(qk_t[:, g].rearrange("p a t -> p (a t)"), bank,
                                     ACT.Copy).then_inc(stack_kept, 1)

            def exponentials(g, half, n):
                act.wait_ge(s2_done[half], n + 1)
                if not (isinstance(n, int) and n == 0):
                    act.wait_ge(low_done[half], n)
                    act.wait_ge(pv_done[half], after(n - 1))
                src = s2[half][:, :, 0:SCORE_COLS]
                nc.scalar.activation(probs[half][:], src, ACT.Exp)
                nc.scalar.activation(p_high[g % 2][half][:], src, ACT.Exp)\
                    .then_inc(exp_done[half], 1)

            for g, bank in enumerate((misc, banks[:, 2], banks[:, 3], banks[:, 4])):
                keep_stack(g, bank, g + 1)
            for half in range(2):
                exponentials(0, half, 0)

            def keep_sums(g, b, n):
                act.wait_ge(pv_done[1], after(n + 1))
                act.wait_ge(pv_turned[g // 2], after(b))
                nc.scalar.activation(o_t[:, g, :], pv[0:VROWS, 0:SEQ], ACT.Copy)\
                    .then_inc(pv_kept, 1)

            def sequence(b, last_one):
                for g in range(GROUPS):
                    n = 4 * b + g
                    if last_one and g == GROUPS - 1:
                        silu_unit(0, 0)
                        keep_sums(g, b, n)
                        silu_unit(1, 0)
                    elif g == GROUPS - 1:
                        exponentials(g + 1, 0, n + 1)
                        keep_sums(g, b, n)
                        exponentials(g + 1, 1, n + 1)
                    else:
                        exponentials(g + 1, 0, n + 1)
                        exponentials(g + 1, 1, n + 1)
                        keep_sums(g, b, n)
                    if last_one and g < 3:
                        act.wait_ge(w_in, 48)
                        nc.scalar.activation(wh[0][g][:], w_sb[g][:, 0:FFN], ACT.Copy)\
                            .then_inc(w_first_high, 1)
                    if not last_one:
                        keep_stack(g, misc, n + GROUPS + 1)
                    if last_one and g in (1, 2):
                        keep_x(g - 1)

            def keep_x(piece):
                act.wait_ge(x_turned, piece + 1)
                lo, hi = X_PIECES[piece]
                nc.scalar.activation(xh[:, lo * P:hi * P], misc[:, 0:(hi - lo) * P],
                                     ACT.Copy).then_inc(xh_ready, 1)

            def silu_unit(k, pair):
                act.wait_ge(up_done, after(UNITS * pair + k + 1))
                act.wait_ge(mul_done[k % 2], after(UNITS // 2 * pair + k // 2))
                nc.scalar.activation(silu[k % 2][:], g_ps[k % 2], ACT.Silu)\
                    .then_inc(silu_done[k % 2], 1)

            def high_unit(k, pair):
                act.wait_ge(mul_done[k % 2], after(UNITS // 2 * pair + k // 2 + 1))
                act.wait_ge(down_done[k % 4], after(UNITS // 4 * pair + k // 4))
                nc.scalar.activation(hh[k % 4][:], hid[k % 2][:], ACT.Copy)\
                    .then_inc(hh_done[k % 4], 1)

            with act.Fori(0, LAST) as b:
                sequence(b, False)
            sequence(LAST, True)

            high_unit(0, 0)
            keep_x(2)
            act.wait_ge(shifted, 1)
            nc.scalar.activation(prob[:], logits[:], ACT.Exp).then_inc(gate_exp, 1)
            with act.Fori(0, PAIRS - 1) as pair:
                for k in range(UNITS):
                    silu_unit(k + 2, pair)
                    high_unit(k + 1, pair)
            pair = PAIRS - 1
            for k in range(UNITS):
                if k + 2 < UNITS:
                    silu_unit(k + 2, pair)
                if k + 1 < UNITS:
                    high_unit(k + 1, pair)

        @block.gpsimd
        def _(pool):
            for s in (*hl_done, *summed):
                pool.sem_inc(s, 1)

            pool_steps = [0]

            def link(ins, base=0):
                pool_steps[0] += 1
                ins.then_inc(pool_chain, 1)
                pool.wait_ge(pool_chain, base + pool_steps[0])

            def none(n):
                return zeros[:, 0:n * HEAD_DIM].rearrange("p (n c) -> p n c", c=HEAD_DIM)

            k_src = k_in[:].rearrange("p n (h c) -> p (n h) c", c=HEAD_DIM)

            def low_keys():
                nc.gpsimd.tensor_tensor(k_rows[:, :, 1, :].bitcast(F32R), k_src,
                                        k_rows[:, :, 0, :], ALU.subtract).then_inc(k_nat_ready, 1)

            def keys(b, base):
                pool.wait_ge(k_loaded, 16 * b + 16)
                nc.gpsimd.tensor_tensor(k_rows[:, :, 2, :].bitcast(F32R), k_src,
                                        none(TPB * HEADS), ALU.add)
                link(nc.gpsimd.tensor_tensor(k_rows[:, :, 0, :].bitcast(F32R), k_src,
                                             none(TPB * HEADS), ALU.add), base)
                low_keys()

            def parts(t, grp, low):
                first = (t * HEADS + grp * HALF) * VROWS + (VHIGH if low else 0)
                flat = v_pad[:, first:first + 4 * (VROWS + VCOLS)]\
                    .rearrange("p (h c) -> p h c", c=VROWS + VCOLS)[:, :, 0:VCOLS]
                flat2 = v_pad[:, first + 4 * VROWS:first + 4 * VROWS + 4 * (VROWS + VCOLS)]\
                    .rearrange("p (h c) -> p h c", c=VROWS + VCOLS)[:, :, 0:VCOLS]
                return flat, flat2

            def value_columns(b, grp, base):
                pool.wait_ge(v_loaded, 16 * b + 16)
                for low in (False, True):
                    for t in range(TPB):
                        for i, dst in enumerate(parts(t, grp, low)):
                            at = (2 * grp + i) * 4 * HEAD_DIM
                            src = v_in[:, t, at:at + 4 * HEAD_DIM]\
                                .rearrange("p (h c) -> p h c", c=HEAD_DIM)
                            if low:
                                last = nc.gpsimd.tensor_tensor(
                                    dst[:, :, 0:HEAD_DIM], src,
                                    parts(t, grp, False)[i][:, :, 0:HEAD_DIM].bitcast(F32),
                                    ALU.subtract)
                            else:
                                last = nc.gpsimd.tensor_tensor(dst[:, :, 0:HEAD_DIM], src,
                                                               none(4), ALU.add)
                    if not low:
                        link(last, base)
                last.then_inc(v_ready[grp], 1)

            def low_probs(g, n):
                pool.wait_ge(exp_done[0], after(n + 1))
                nc.gpsimd.tensor_tensor(p_low[g % 2][0][:], probs[0][:],
                                        p_high[g % 2][0][:].bitcast(F32), ALU.subtract)\
                    .then_inc(low_done[0], 1)

            def inverse_root(tiles, count):
                pool.wait_ge(var_ready, count)
                nc.gpsimd.tensor_tensor(rstd[:, tiles], veps[:, tiles], power[:, tiles], ALU.pow)\
                    .then_inc(rstd_ready, 1)

            nc.gpsimd.memset(power[:], -0.5)
            link(nc.gpsimd.memset(zeros[:], 0.0))
            nc.gpsimd.memset(v_pad[:].bitcast(F32), 0.0).then_inc(pool_chain, 1)
            pool_steps[0] += 1
            inverse_root(slice(0, TPB), 1)
            pool.wait_ge(k_high, 1)
            low_keys()
            pool.wait_ge(pool_chain, 2)
            for t in range(TPB):
                for grp in range(2):
                    for dst in parts(t, grp, False):
                        nc.gpsimd.memset(dst[:, :, HEAD_DIM:VCOLS].bitcast(F32), 1.0)
            value_columns(0, 0, 0)
            low_probs(0, 0)
            value_columns(0, 1, 0)
            inverse_root(slice(TPB, TILES), 2)
            nc.gpsimd.memset(acc[:], 0.0)

            def sequence(b, last_one, base):
                for g in range(GROUPS):
                    n = 4 * b + g
                    if not last_one and g == 0:
                        pool.wait_ge(stacked, n + GROUPS)
                        keys(b + 1, base)
                    if not (last_one and g == GROUPS - 1):
                        low_probs(g + 1, n + 1)
                    if not last_one and g % 2:
                        pool.wait_ge(pv_done[1], after(n + 1))
                        value_columns(b + 1, g // 2, base)
                    if last_one and g == 0:
                        inverse_root(slice(0, TPB * LAST), 3)
                    if last_one and g < 3:
                        pool.wait_ge(w_first_high, g + 1)
                        nc.gpsimd.tensor_tensor(wl[0][g][:], w_sb[g][:, 0:FFN],
                                                wh[0][g][:].bitcast(F32), ALU.subtract)\
                            .then_inc(w_first, 1)

            before = pool_steps[0]
            with pool.Fori(0, LAST) as b:
                pool_steps[0] = before
                sequence(b, False, 3 * b)
            assert pool_steps[0] == before + 3
            sequence(LAST, True, 0)
            inverse_root(slice(TPB * LAST, TILES), 4)

            def low_unit(k, pair):
                pool.wait_ge(hh_done[k % 4], UNITS // 4 * pair + k // 4 + 1)
                pool.wait_ge(down_done[k % 4], after(UNITS // 4 * pair + k // 4))
                nc.gpsimd.tensor_tensor(hl[k % 4][:], hid[k % 2][:], hh[k % 4][:].bitcast(F32),
                                        ALU.subtract).then_inc(hl_done[k % 4], 1)

            def add_chunk(c, count):
                pool.wait_ge(scaled[c], after(count))
                pool.wait_ge(summed[c], after(count - 1))
                nc.gpsimd.tensor_tensor(acc[:, c, :], acc[:, c, :], part[c][:], ALU.add)\
                    .then_inc(summed[c], 1)

            def experts(pair, last_one):
                for k in range(UNITS):
                    if not (last_one and k + LAG + 2 >= UNITS):
                        low_unit(k + LAG + 2, pair)
                    if k % FT == FT - 1:
                        add_chunk(k // FT % CHUNKS, 2 * pair + k // (FT * CHUNKS) + 1)

            for k in range(LAG + 2):
                low_unit(k, 0)
            with pool.Fori(0, PAIRS - 1) as pair:
                experts(pair, False)
            experts(PAIRS - 1, True)

        @block.vector
        def _(dve):
            for s in (*attn_done, *mul_done, *scaled):
                dve.sem_inc(s, 1)

            steps = [0]

            def link(ins, base=0):
                steps[0] += 1
                ins.then_inc(dve_chain, 1)
                dve.wait_ge(dve_chain, base + steps[0])

            for i in range(2):
                dve.sem_inc(w_split[i], 1)
            var = stats[:].rearrange("p (t c) -> p t c", c=2)[:, :, 1]

            def moments(src, tiles, scale, base):
                for t in tiles:
                    last = nc.vector.bn_stats(bn[:, t, :], src[:, t, :])
                link(last, base)
                for t in tiles:
                    last = nc.vector.bn_aggr(stats[:, 2 * t:2 * t + 2], bn[:, t, :])
                link(last, base)
                at = slice(tiles[0], tiles[-1] + 1)
                nc.vector.tensor_scalar(veps[:, at], var[:, at], EPS, scale, ALU.add, ALU.mult)\
                    .then_inc(var_ready, 1)

            nc.vector.memset(max_nat[:], 0.0)
            dve.wait_ge(first_in, 16)
            moments(x_in, range(0, TPB), float(HEAD_DIM), 0)
            dve.wait_ge(const_in, 16)
            nc.vector.tensor_copy(q_nat[:, :, QK_COLS:ROWS], q_const)
            nc.vector.tensor_copy(cb[:].rearrange("p a n -> p (a n)"), cf[:, 0:3 * P])\
                .then_inc(masks_ready, 1)
            dve.wait_ge(rstd_ready, 1)

            def queries(b_next, base):
                for t in range(TPB):
                    at = TPB * b_next + t
                    last = nc.vector.tensor_scalar(
                        q_norm[:, t, :], x_in[:, ds(at, 1), :].rearrange("p a d -> p (a d)"),
                        stats[:, ds(2 * at, 1)], rstd[:, ds(at, 1)],
                        ALU.subtract, ALU.mult)
                link(last, base)
                src = q_norm[:].rearrange("p n (h c) -> p (n h) c", c=HEAD_DIM)
                rows = q_nat[:, :, 0:QK_COLS].rearrange("p n (r c) -> p n r c", c=HEAD_DIM)
                link(nc.vector.tensor_copy(
                    rows[:, :, 0:2, :].bitcast(F32R),
                    src.unsqueeze(2).broadcast_to([P, TPB * HEADS, 2, HEAD_DIM])), base)
                nc.vector.tensor_tensor(rows[:, :, 2, :].bitcast(F32R), src, rows[:, :, 0, :],
                                        ALU.subtract).then_inc(q_nat_ready, 1)

            def maxima(half, count, s1=s1):
                if half == 0 and not (isinstance(count, int) and count == 1):
                    dve.wait_ge(max_split, count - 1)
                dve.wait_ge(s1_done[half], count)
                hs = slice(2 * half, 2 * half + 2)
                nc.vector.tensor_reduce(neg_max[:, 0, hs], s1[:, :, 0:P], AX.X, ALU.max,
                                        negate=True)
                return nc.vector.tensor_reduce(neg_max[:, 1, hs], s1[:, :, P:P + SEQ], AX.X,
                                               ALU.max, negate=True).then_inc(max_done[half], 1)

            def split_maxima(base, count):
                if not (isinstance(count, int) and count == 1):
                    dve.wait_ge(max_turned, count - 1)
                dve.wait_ge(max_done[0], count)
                dve.wait_ge(max_done[1], count)
                link(nc.vector.tensor_copy(max_nat[:, :, :, MAX_COL].bitcast(F32R), neg_max[:]),
                     base)
                nc.vector.tensor_tensor(max_nat[:, :, :, MAX_COL + 1].bitcast(F32R), neg_max[:],
                                        max_nat[:, :, :, MAX_COL], ALU.subtract)\
                    .then_inc(max_split, 1)

            def place_maxima(g, count):
                dve.wait_ge(max_turned, count)
                dve.wait_ge(stack_kept, count)
                nc.vector.tensor_tensor(q_max_t[:, g, :], misc[:, 0:SEQ],
                                        qk_t[:, g, 0, :].bitcast(F32), ALU.add)\
                    .then_inc(q_max_ready, 1)

            def finish_heads(b, grp, base, turned):
                dve.wait_ge(pv_turned[grp], after(b + 1))
                o = turned.rearrange("p t (h c) -> p t h c", c=VCOLS)
                link(nc.vector.reciprocal(r_den[:], o[:, :, :, HEAD_DIM]), base)
                nc.vector.tensor_tensor(
                    attn[:], o[:, :, :, 0:HEAD_DIM],
                    r_den[:].unsqueeze(3).broadcast_to([P, TPB, HALF, HEAD_DIM]), ALU.mult)\
                    .then_inc(attn_done[grp], 1)

            def add_residual(b, grp):
                dve.wait_ge(attn_done[grp], after(b + 1))
                cols = slice(grp * HALF * HEAD_DIM, (grp + 1) * HALF * HEAD_DIM)
                return nc.vector.tensor_tensor(
                    x_mid[:, ds(TPB * b, TPB), cols], attn[:].rearrange("p t h c -> p t (h c)"),
                    x_in[:, ds(TPB * b, TPB), cols], ALU.add)

            def low_probs(g, n):
                dve.wait_ge(exp_done[1], after(n + 1))
                nc.vector.tensor_tensor(p_low[g % 2][1][:], probs[1][:],
                                        p_high[g % 2][1][:].bitcast(F32), ALU.subtract)\
                    .then_inc(low_done[1], 1)

            queries(0, 0)
            for n in range(3):
                maxima(0, n + 1, first_s1[n][0])
                if n:
                    place_maxima(n - 1, n)
                maxima(1, n + 1, first_s1[n][1])
                split_maxima(0, n + 1)
            dve.wait_ge(rest_in, 16)
            moments(x_in, range(TPB, TILES), float(HEAD_DIM), 0)
            dve.wait_ge(rstd_ready, 2)

            def x_mid_normalised(tiles, count):
                dve.wait_ge(rstd_ready, count)
                for t in tiles:
                    last = nc.vector.tensor_scalar(x_norm[:, t, :], x_mid[:, t, :],
                                                   stats[:, 2 * t:2 * t + 1], rstd[:, t:t + 1],
                                                   ALU.subtract, ALU.mult)
                    if t in (3, 5, 7):
                        last.then_inc(x_norm_ready, 1)

            def low_x(piece):
                dve.wait_ge(xh_ready, piece + 1)
                lo, hi = X_PIECES[piece]
                nc.vector.tensor_tensor(xl[:, lo * P:hi * P], misc[:, 0:(hi - lo) * P],
                                        xh[:, lo * P:hi * P].bitcast(F32),
                                        ALU.subtract).then_inc(xl_ready, 1)

            def keep_logits():
                dve.wait_ge(logits_done, 1)
                nc.vector.tensor_tensor(
                    logits[:],
                    misc[:, SEQ:SEQ + TILES * EXPERTS].rearrange("p (t e) -> p t e", e=EXPERTS),
                    bias_sb[:].unsqueeze(1).broadcast_to([P, TILES, EXPERTS]), ALU.add)\
                    .then_inc(logits_kept, 1)

            def sequence(b, last_one, per):
                base = per * b
                for g in range(GROUPS):
                    n = 4 * b + g
                    more = [not last_one or g + ahead < GROUPS for ahead in range(4)]
                    low_probs(g, n)
                    if last_one and g == 2:
                        low_x(0)
                    if last_one and g == 3:
                        low_x(1)
                        multiply(0, 0)
                    if more[3]:
                        if not last_one and g == 2:
                            dve.wait_ge(pv_turned[0], after(b + 1))
                        maxima(0, n + 4)
                    if more[2]:
                        place_maxima((g + 2) % GROUPS, n + 3)
                    if not last_one and g == 0:
                        dve.wait_ge(stacked, 4 * b + GROUPS)
                        queries(b + 1, base)
                    if g >= 2:
                        finish_heads(b, g - 2, base, in_misc if last_one else by_scores)
                    if more[3]:
                        maxima(1, n + 4)
                        split_maxima(base, n + 4)
                    if g >= 2:
                        last = add_residual(b, g - 2)
                    if last_one and g == 0:
                        moments(x_mid, range(TPB * LAST), 1.0, base)
                    if last_one and g == 1:
                        x_mid_normalised(range(TPB * LAST), 3)
                        dve.wait_ge(gate_in, 32)
                        link(nc.vector.tensor_copy(gate_hl[:, 0, :], gate_sb[:]), base)
                        nc.vector.tensor_tensor(gate_hl[:, 1, :], gate_sb[:],
                                                gate_hl[:, 0, :].bitcast(F32),
                                                ALU.subtract).then_inc(gate_ready, 1)
                return last

            def multiply(k, pair):
                dve.wait_ge(silu_done[k % 2], after(UNITS // 2 * pair + k // 2 + 1))
                dve.wait_ge(hl_done[(k - 2) % 4],
                            after(UNITS // 4 * pair + (k - 2) // 4 + 1))
                nc.vector.tensor_tensor(hid[k % 2][:], silu[k % 2][:], u_ps[k % 2], ALU.mult)\
                    .then_inc(mul_done[k % 2], 1)

            before = steps[0]
            PER = 8
            with dve.Fori(0, LAST) as b:
                steps[0] = before
                sequence(b, False, PER)
            assert steps[0] - before == PER, steps[0] - before
            steps[0] = before
            base = PER * LAST
            link(sequence(LAST, True, PER), base)

            moments(x_mid, range(TPB * LAST, TILES), 1.0, base)
            multiply(1, 0)
            x_mid_normalised(range(TPB * LAST, TILES), 4)
            low_x(2)
            keep_logits()
            dve.wait_ge(logits_kept, 1)

            def split_weights(i, m, e, count):
                src = w_sb[m][:, ds(e * FFN, FFN)]
                ins = nc.vector.tensor_copy(wh[i][m][:], src)
                ins.then_inc(w_high, 1)
                dve.wait_ge(w_high, count)
                nc.vector.tensor_tensor(wl[i][m][:], src, wh[i][m][:].bitcast(F32),
                                        ALU.subtract).then_inc(w_split[i], 1)

            link(nc.vector.tensor_reduce(row[:], logits[:], AX.X, ALU.max), base)
            nc.vector.tensor_tensor(logits[:], logits[:],
                                    row[:].unsqueeze(2).broadcast_to([P, TILES, EXPERTS]),
                                    ALU.subtract).then_inc(shifted, 1)
            multiply(2, 0)
            dve.wait_ge(gate_exp, 1)
            link(nc.vector.tensor_reduce(row[:], prob[:], AX.X, ALU.add), base)
            link(nc.vector.reciprocal(row[:], row[:]), base)
            link(nc.vector.tensor_tensor(prob[:], prob[:],
                                         row[:].unsqueeze(2).broadcast_to([P, TILES, EXPERTS]),
                                         ALU.mult), base)
            for t in range(TILES):
                last = nc.vector.max(top[:, t, :], prob[:, t, :])
            link(last, base)
            link(nc.vector.tensor_tensor(row[:], top[:, :, 0], top[:, :, 1], ALU.add), base)
            link(nc.vector.memset(top[:, :, TOP_K:], -1.0), base)
            for t in range(TILES):
                nc.vector.match_replace(rest[:, t, :], top[:, t, :], prob[:, t, :], 0.0)
            link(nc.vector.reciprocal(row[:], row[:]), base)
            link(nc.vector.tensor_tensor(prob[:], prob[:], rest[:], ALU.subtract), base)
            link(nc.vector.tensor_tensor(comb[:].rearrange("p e t -> p t e"), prob[:],
                                         row[:].unsqueeze(2).broadcast_to([P, TILES, EXPERTS]),
                                         ALU.mult), base)
            nc.vector.transpose(comb_t[:], comb[:].rearrange("p e t -> p (e t)"))\
                .then_inc(comb_turned, 1)

            def scale(k, pair):
                i, c = k // (CHUNKS * FT), k // FT % CHUNKS
                dve.wait_ge(down_done[k % 4], after(UNITS // 4 * pair + k // 4 + 1))
                dve.wait_ge(comb_in[i], 16 * (pair + 1))
                dve.wait_ge(summed[c], after(2 * pair + i))
                nc.vector.tensor_tensor(part[c][:], d_ps[c],
                                        comb_all[i][:, c * CHUNK:(c + 1) * CHUNK], ALU.mult)\
                    .then_inc(scaled[c], 1)

            def experts(pair, last_one):
                count = 6 * pair
                for k in range(UNITS):
                    if k < 2:
                        dve.wait_ge(up_done, after(UNITS * pair))
                        split_weights(1, k, 2 * pair + 1, count + k + 1)
                    if k == 2:
                        dve.wait_ge(down_done[3], after(UNITS // 4 * pair))
                        split_weights(1, k, 2 * pair + 1, count + k + 1)
                    if not last_one and k in (6, 7):
                        dve.wait_ge(up_done, after(UNITS * pair + UNITS // 2))
                        split_weights(0, k - 6, 2 * pair + 2, count + k - 6 + 4)
                    if not last_one and k == 8:
                        dve.wait_ge(down_done[3], after(UNITS // 4 * pair + UNITS // 8))
                        split_weights(0, k - 6, 2 * pair + 2, count + k - 6 + 4)
                    if not (last_one and k + LAG + 1 >= UNITS):
                        multiply(k + LAG + 1, pair)
                    if k % FT == FT - 1:
                        scale(k, pair)

            for k in range(3, LAG + 1):
                multiply(k, 0)
            with dve.Fori(0, PAIRS - 1) as pair:
                experts(pair, False)
            experts(PAIRS - 1, True)

            half = TILES // 2
            for c in range(CHUNKS):
                dve.wait_ge(y_turned, c + 1)
                nc.vector.tensor_tensor(
                    y[:, c * half:(c + 1) * half, :].rearrange("p t d -> p (t d)"),
                    banks[:, 6 + c, :],
                    x_mid[:, c * half:(c + 1) * half, :].rearrange("p t d -> p (t d)"),
                    ALU.add).then_inc(y_ready, 1)


_INS = ["x", "ctx_1024", "L0_ffn_gate_w", "L0_ffn_gate_b", "L0_ffn_w1", "L0_ffn_w3", "L0_ffn_w2"]


def kernel(**inputs):
    import concourse.bacc as bacc
    from concourse.bass_utils import run_bass_kernel_spmd

    nc = bacc.Bacc("TRN2", target_bir_lowering=False, num_devices=1)
    arrays = {name: np.ascontiguousarray(inputs[name]) for name in _INS}
    for name in ("x", "ctx_1024", "L0_ffn_w2"):
        arrays[name] = arrays[name].reshape(-1, D)
    arrays["consts"] = constants()
    arrays = {f"in_{name}": a for name, a in arrays.items()}
    args = [nc.dram_tensor(name, a.shape, mybir.dt.from_np(a.dtype), kind="ExternalInput").ap()
            for name, a in arrays.items()]
    out = nc.dram_tensor("out", (TOKENS, D), mybir.dt.float32, kind="ExternalOutput").ap()
    c_dram = nc.dram_tensor("c_dram", (EXPERTS * TILES, P), mybir.dt.float32, kind="Internal").ap()
    build(nc, *args, out, c_dram)
    r = run_bass_kernel_spmd(nc, [arrays], core_ids=[0])
    return r.results[0]["out"].reshape(BATCH, SEQ, D)
```

```python
from contextlib import ExitStack

import numpy as np
import concourse.bass as bass
from concourse import mybir

P = 128
BATCH, SEQ, D = 4, 256, 128
HEADS, HEAD_DIM = 16, 8
EXPERTS, FFN, TOP_K = 8, 512, 2
EPS = 1e-5

TILES = BATCH * SEQ // P
TPB = SEQ // P
GROUPS = HEADS // 4
ROWS = 32
QK_COLS = 3 * HEAD_DIM
MAX_COL = QK_COLS + 4
VCOLS = HEAD_DIM + 1
VHIGH = 4 * VCOLS
VROWS = 2 * VHIGH
HALF = HEADS // 2
SCORE_COLS = SEQ + P
FT = FFN // P
TOKENS = BATCH * SEQ
CHUNK = 512
CHUNKS = TOKENS // CHUNK
UNITS = 2 * CHUNKS * FT
LAG = 4


def constants():
    def high(a):
        bits = np.ascontiguousarray(a, np.float32).view(np.uint32).astype(np.uint64)
        return ((bits + 0x800) & 0xFFFFF000).astype(np.uint32).view(np.float32)

    slope = np.cumprod(np.full(HEADS, 2.0 ** (-8.0 / HEADS), np.float32), dtype=np.float32)
    token = np.arange(SEQ, dtype=np.float32).reshape(TPB, P).T[:, :, None]
    q = np.zeros((P, TPB, HEADS, 8), np.float32)
    k = np.zeros((P, TPB, HEADS, 8), np.float32)
    down = (-token * slope).astype(np.float32)
    q[..., 0], q[..., 1] = high(slope), slope - high(slope)
    q[..., 2], q[..., 3] = high(down), down - high(down)
    k[..., 0] = k[..., 1] = token
    k[..., 2:6] = 1.0
    p = np.arange(P)
    fold = (p[:, None] % VHIGH == np.arange(VHIGH)) & (p[:, None] < VROWS)
    return np.concatenate([np.eye(P), np.where(p[None, :] > p[:, None], -1e30, 0.0),
                           np.where(p[:, None] > p[None, :], -1e30, 0.0),
                           q.reshape(P, -1), k.reshape(P, -1), fold], 1).astype(np.float32)


def build(nc, x, ctx_in, gate_w, gate_b, w1, w3, w2, consts, out, c_dram):
    F32, F32R, BF16 = mybir.dt.float32, mybir.dt.float32r, mybir.dt.bfloat16
    ALU, ACT, AX = mybir.AluOpType, mybir.ActivationFunctionType, mybir.AxisListType
    ds = bass.ds

    with ExitStack() as stack:
        def sb(name, shape, dt=F32):
            return stack.enter_context(nc.sbuf_tensor(name, shape, dt))

        def sem(name):
            return stack.enter_context(nc.semaphore(name))

        n_const = TPB * HEADS * 8
        cf = sb("cf", [P, 3 * P + 2 * n_const + VHIGH])
        ident = cf[:, 0:P]
        q_const = cf[:, 3 * P:3 * P + n_const].rearrange("p (n c) -> p n c", c=8)
        k_const = cf[:, 3 * P + n_const:3 * P + 2 * n_const].rearrange("p (n c) -> p n c", c=8)
        fold = cf[0:VROWS, 3 * P + 2 * n_const:]
        cb = sb("cb", [P, 3, P], BF16)
        x_in = sb("x_in", [P, TILES, D])
        k_in = sb("k_in", [P, TPB, D])
        v_in = sb("v_in", [P, TPB, D])
        gate_sb = sb("gate_sb", [P, EXPERTS])
        bias_sb = sb("bias_sb", [P, EXPERTS])
        w1_sb = sb("w1_sb", [P, EXPERTS * FFN])
        w3_sb = sb("w3_sb", [P, EXPERTS * FFN])
        w2_sb = sb("w2_sb", [P, EXPERTS * FFN])
        bn = sb("bn", [P, TILES, 6])
        stats = sb("stats", [P, TILES * 2])
        veps = sb("veps", [P, TILES])
        power = sb("power", [P, TILES])
        rstd = sb("rstd", [P, TILES])
        q_nat = sb("q_nat", [P, TPB * HEADS, ROWS])
        k_nat = sb("k_nat", [P, TPB * HEADS, ROWS])
        qk_t = sb("qk_t", [P, GROUPS, 2, SEQ], F32R)
        q_max_t = sb("q_max_t", [P, GROUPS, SEQ], F32R)
        neg_max = sb("neg_max", [P, TPB, 4])
        max_nat = sb("max_nat", [P, TPB, 4, ROWS])
        zeros = sb("zeros", [P, TPB * D])
        v_pad = sb("v_pad", [P, TPB * HEADS * VROWS + VROWS], F32R)
        probs = [sb(f"probs{i}", [P, 2, SCORE_COLS]) for i in range(2)]
        p_high = [[sb(f"p_high{i}{h}", [P, 2, SCORE_COLS], F32R) for h in range(2)]
                  for i in range(2)]
        p_low = [[sb(f"p_low{i}{h}", [P, 2, SCORE_COLS], F32R) for h in range(2)]
                 for i in range(2)]
        o_t = sb("o_t", [VROWS, GROUPS, SEQ])
        r_den = sb("r_den", [P, TPB, HALF])
        attn = sb("attn", [P, TPB, HALF, HEAD_DIM])
        x_mid = sb("x_mid", [P, TILES, D])
        x_norm = sb("x_norm", [P, TILES, D])
        xh = sb("xh", [P, TOKENS], F32R)
        xl = sb("xl", [P, TOKENS], F32R)
        gate_hl = sb("gate_hl", [P, 2, EXPERTS], F32R)
        logits = sb("logits", [P, TILES, EXPERTS])
        row = sb("row", [P, TILES])
        prob = sb("prob", [P, TILES, EXPERTS])
        top = sb("top", [P, TILES, 8])
        rest = sb("rest", [P, TILES, EXPERTS])
        comb = sb("comb", [P, EXPERTS, TILES])
        comb_t = sb("comb_t", [P, EXPERTS * TILES])
        comb_all = [sb(f"comb_all{i}", [P, TOKENS]) for i in range(2)]
        wh = [[sb(f"wh{m}_{i}", [P, FFN], F32R) for m in range(3)] for i in range(2)]
        wl = [[sb(f"wl{m}_{i}", [P, FFN], F32R) for m in range(3)] for i in range(2)]
        silu = [sb(f"silu{i}", [P, CHUNK]) for i in range(2)]
        hid = [sb(f"hid{i}", [P, CHUNK]) for i in range(2)]
        hh = [sb(f"hh{i}", [P, CHUNK], F32R) for i in range(4)]
        hl = [sb(f"hl{i}", [P, CHUNK], F32R) for i in range(4)]
        part = [sb(f"part{i}", [P, CHUNK]) for i in range(2)]
        acc = sb("acc", [P, CHUNKS, CHUNK])
        y = x_norm

        banks = stack.enter_context(nc.psum_tensor("banks", [P, 8, 512], F32))
        s1 = banks[:, 0:2]
        s2 = [banks[:, 2:4], banks[:, 4:6]]
        pv = banks[:, 6]
        misc = banks[:, 7]
        g_ps = [banks[:, 0], banks[:, 1]]
        u_ps = [banks[:, 2], banks[:, 3]]
        d_ps = [banks[:, 4], banks[:, 5]]

        k_rows = k_nat[:, :, 0:QK_COLS].rearrange("p n (r c) -> p n r c", c=HEAD_DIM)
        w_sb = (w1_sb, w3_sb, w2_sb)

        first_s1 = ((s1, banks[:, 5:7]), (banks[:, 2:4], s1), (banks[:, 5:7], s1))
        by_sums = pv[:, SEQ:SEQ + TPB * VROWS].rearrange("p (t c) -> p t c", t=TPB)
        in_misc = misc[:, 0:TPB * VROWS].rearrange("p (t c) -> p t c", t=TPB)

        def diagonal(bank):
            return bank.rearrange("p (a b) -> p a b", b=SEQ)[:, :, 0:P]

        const_in = sem("const_in")
        first_in = sem("first_in")
        k_loaded = sem("k_loaded")
        v_loaded = sem("v_loaded")
        rest_in = sem("rest_in")
        gate_in = sem("gate_in")
        w_first_in = sem("w_first_in")
        w_in = sem("w_in")
        comb_out = sem("comb_out")
        comb_in = [sem(f"comb_in{i}") for i in range(2)]
        out_sem = sem("out_sem")
        dve_chain = sem("dve_chain")
        pool_chain = sem("pool_chain")
        masks_ready = sem("masks_ready")
        var_ready = sem("var_ready")
        rstd_ready = sem("rstd_ready")
        q_nat_ready = sem("q_nat_ready")
        k_nat_ready = sem("k_nat_ready")
        v_ready = [sem(f"v_ready{i}") for i in range(2)]
        stacked = sem("stacked")
        stack_kept = sem("stack_kept")
        s1_done = [sem(f"s1_done{i}") for i in range(2)]
        max_done = [sem(f"max_done{i}") for i in range(2)]
        max_split = sem("max_split")
        max_turned = sem("max_turned")
        q_max_ready = sem("q_max_ready")
        s2_done = [sem(f"s2_done{i}") for i in range(2)]
        exp_done = [sem(f"exp_done{i}") for i in range(2)]
        low_done = [sem(f"low_done{i}") for i in range(2)]
        pv_done = [sem(f"pv_done{i}") for i in range(2)]
        pv_kept = sem("pv_kept")
        pv_turned = [sem(f"pv_turned{i}") for i in range(2)]
        attn_done = [sem(f"attn_done{i}") for i in range(2)]
        x_norm_ready = sem("x_norm_ready")
        x_turned = sem("x_turned")
        xh_ready = sem("xh_ready")
        xl_ready = sem("xl_ready")
        gate_ready = sem("gate_ready")
        logits_done = sem("logits_done")
        shifted = sem("shifted")
        gate_exp = sem("gate_exp")
        logits_kept = sem("logits_kept")
        comb_turned = sem("comb_turned")
        k_high = sem("k_high")
        w_first_high = sem("w_first_high")
        w_first = sem("w_first")
        w_high = sem("w_high")
        w_split = [sem(f"w_split{i}") for i in range(2)]
        up_done = sem("up_done")
        silu_done = [sem(f"silu_done{i}") for i in range(2)]
        mul_done = [sem(f"mul_done{i}") for i in range(2)]
        hh_done = [sem(f"hh_done{i}") for i in range(4)]
        hl_done = [sem(f"hl_done{i}") for i in range(4)]
        down_done = [sem(f"down_done{i}") for i in range(4)]
        scaled = [sem(f"scaled{i}") for i in range(2)]
        summed = [sem(f"summed{i}") for i in range(2)]
        y_turned = sem("y_turned")
        y_ready = sem("y_ready")

        def after(n):
            return n + 1

        block = stack.enter_context(nc.Block())

        X_PIECES = ((0, 4), (4, 8))
        FIRST_WEIGHTS = ((0, 0), (0, 1), (0, 2), (1, 0), (1, 1))
        LAST = BATCH - 1
        PAIRS = EXPERTS // 2

        @block.sync
        def _(sp):
            tiled = lambda a: a.rearrange("(n p) d -> p n d", p=P)
            sp.dma_start(x_in[:, 0:TPB], tiled(x)[:, 0:TPB]).then_inc(first_in, 16)
            sp.dma_start(k_in[:], tiled(ctx_in)[:, 0:TPB]).then_inc(k_loaded, 16)
            sp.dma_start(v_in[:], tiled(ctx_in)[:, 0:TPB]).then_inc(v_loaded, 16)
            sp.dma_start(x_in[:, TPB:], tiled(x)[:, TPB:]).then_inc(rest_in, 16)
            sp.dma_start(gate_sb[:], gate_w).then_inc(gate_in, 16)
            sp.dma_start(bias_sb[:], gate_b.partition_broadcast(P)).then_inc(gate_in, 16)

            def load_weights(experts, signal):
                for w_sb_, w in ((w1_sb, w1), (w3_sb, w3)):
                    sp.dma_start(w_sb_[:].rearrange("p (e f) -> p e f", e=EXPERTS)[:, experts],
                                 w.rearrange("e d f -> d e f")[:, experts]).then_inc(signal, 16)
                tiles = slice(experts.start * FT, experts.stop * FT)
                sp.dma_start(w2_sb[:].rearrange("p (n d) -> p n d", d=D)[:, tiles],
                             w2.rearrange("(n p) d -> p n d", p=P)[:, tiles]).then_inc(signal, 16)

            def load_keys(b):
                sp.wait_ge(k_nat_ready, b)
                sp.dma_start(k_in[:], tiled(ctx_in)[:, ds(TPB * b, TPB)]).then_inc(k_loaded, 16)

            def load_values(b):
                sp.wait_ge(v_ready[0], b)
                sp.wait_ge(v_ready[1], b)
                sp.dma_start(v_in[:], tiled(ctx_in)[:, ds(TPB * b, TPB)]).then_inc(v_loaded, 16)

            load_weights(slice(0, 2), w_first_in)
            load_keys(1)
            load_weights(slice(2, EXPERTS), w_in)
            with sp.Fori(1, LAST) as b:
                load_values(b)
                load_keys(b + 1)
            load_values(LAST)
            sp.wait_ge(comb_turned, 1)
            for q in range(P // 32):
                sp.dma_start(c_dram[:, 32 * q:32 * q + 32].rearrange("(c i) j -> i c j", i=32),
                             comb_t[32 * q:32 * q + 32, :].rearrange("i (c j) -> i c j", j=32))\
                    .then_inc(comb_out, 16)
            sp.wait_ge(comb_out, 16 * (P // 32))
            rows = c_dram.rearrange("(e n) t -> e (n t)", e=EXPERTS)

            def load_comb(i, e):
                sp.dma_start(comb_all[i][:], rows[ds(e, 1), :].rearrange("a t -> (a t)")
                             .partition_broadcast(P)).then_inc(comb_in[i], 16)

            for i in range(2):
                load_comb(i, i)
            with sp.Fori(1, PAIRS) as pair:
                for i in range(2):
                    for c in range(CHUNKS):
                        sp.wait_ge(scaled[c], after(2 * pair + (i - 1)))
                    load_comb(i, 2 * pair + i)
            flat = tiled(out)
            half = TILES // 2
            for c in range(2):
                sp.wait_ge(y_ready, c + 1)
                sp.dma_start(flat[:, c * half:(c + 1) * half],
                             y[:, c * half:(c + 1) * half]).then_inc(out_sem, 16)
            sp.wait_ge(out_sem, 32)

        @block.tensor
        def _(pe):
            for s in (*pv_done, *pv_turned, up_done, *down_done):
                pe.sem_inc(s, 1)

            def stack_group(g, bank):
                for nat, at in ((q_nat, 0), (k_nat, SEQ)):
                    for t in range(TPB):
                        src = nat[:, t * HEADS + 4 * g:t * HEADS + 4 * g + 4, :]
                        last = nc.tensor.transpose(bank[:, at + t * P:at + (t + 1) * P],
                                                   src.rearrange("p h r -> p (h r)"), ident)
                last.then_inc(stacked, 1)

            def masked(banks_, mask):
                for j in range(2):
                    nc.tensor.matmul(diagonal(banks_[:, j]), cb[:, 0, :],
                                     mask.unsqueeze(1).broadcast_to([P, 2, P]),
                                     start=True, stop=False, skip_group_check=True)

            def rows_of(half, j):
                return slice(ROWS * (2 * half + j), ROWS * (2 * half + j + 1))

            def scores_for_maxima(g, half, s1=s1):
                masked(s1, cb[:, 1, :])
                for j in range(2):
                    q, k = qk_t[rows_of(half, j), g, 0, :], qk_t[rows_of(half, j), g, 1, :]
                    nc.tensor.matmul(s1[:, j, P:P + SEQ], q[:, P:SEQ], k[:, 0:SEQ],
                                     start=False, stop=False, skip_group_check=True)
                for j in range(2):
                    q, k = qk_t[rows_of(half, j), g, 0, :], qk_t[rows_of(half, j), g, 1, :]
                    last = nc.tensor.matmul(s1[:, j, 0:P], q[:, 0:P], k[:, 0:P],
                                            start=False, stop=True, skip_group_check=True)
                last.then_inc(s1_done[half], 1)

            def scores_for_exp(g, half):
                masked(s2[half], cb[:, 2, :])
                for j in range(2):
                    q, k = q_max_t[rows_of(half, j), g, :], qk_t[rows_of(half, j), g, 1, :]
                    nc.tensor.matmul(s2[half][:, j, 0:SEQ], k[:, 0:P], q[:, 0:SEQ],
                                     start=False, stop=False, skip_group_check=True)
                for j in range(2):
                    q, k = q_max_t[rows_of(half, j), g, :], qk_t[rows_of(half, j), g, 1, :]
                    last = nc.tensor.matmul(s2[half][:, j, SEQ:SEQ + P], k[:, P:SEQ], q[:, P:SEQ],
                                            start=False, stop=True, skip_group_check=True)
                last.then_inc(s2_done[half], 1)

            def values(g, half):
                sums = pv[0:VROWS, 0:SEQ]
                for j in range(2):
                    h = 4 * g + 2 * half + j
                    first, final = 2 * half + j == 0, 2 * half + j == 3
                    for t, cols, to in ((0, slice(0, SEQ), sums),
                                        (1, slice(SEQ, SEQ + P), sums[:, P:SEQ])):
                        own = v_pad[:, (t * HEADS + h) * VROWS:(t * HEADS + h + 1) * VROWS]
                        nc.tensor.matmul(to, own, p_high[g % 2][half][:, j, cols],
                                         start=first and t == 0, stop=False,
                                         skip_group_check=True)
                        last = nc.tensor.matmul(to, own, p_low[g % 2][half][:, j, cols],
                                                start=False, stop=final and t == 1,
                                                skip_group_check=True)
                last.then_inc(pv_done[half], 1)

            def turn_max():
                for t in range(TPB):
                    last = nc.tensor.transpose(misc[:, t * P:(t + 1) * P],
                                               max_nat[:, t].rearrange("p h r -> p (h r)"), ident)
                last.then_inc(max_turned, 1)

            def turn_values(grp, to):
                for t in range(TPB):
                    for i in range(2):
                        last = nc.tensor.matmul(to[:, t, i * VHIGH:(i + 1) * VHIGH],
                                                o_t[:, 2 * grp + i, t * P:(t + 1) * P], fold,
                                                start=True, stop=True)
                last.then_inc(pv_turned[grp], 1)

            def turn_x(tiles):
                for i, t in enumerate(tiles):
                    last = nc.tensor.transpose(misc[:, i * P:(i + 1) * P], x_norm[:, t, :], ident)
                last.then_inc(x_turned, 1)

            zeros_b = zeros[:, 0:P // 2].bitcast(BF16)

            def keep_clock(count):
                for _ in range(count):
                    nc.tensor.matmul(banks[:, 4, SCORE_COLS:], zeros_b, zeros_b,
                                     start=True, stop=True, skip_group_check=True)

            pe.wait_ge(pool_chain, 1)
            keep_clock(48)
            pe.wait_ge(const_in, 16)
            pe.wait_ge(q_nat_ready, 1)
            pe.wait_ge(k_nat_ready, 1)
            stack_group(0, misc)
            stack_group(1, banks[:, 2])
            pe.wait_ge(masks_ready, 1)
            pe.wait_ge(stack_kept, 1)
            scores_for_maxima(0, 0)
            stack_group(2, banks[:, 3])
            stack_group(3, banks[:, 4])
            scores_for_maxima(0, 1, first_s1[0][1])
            pe.wait_ge(stack_kept, 3)
            scores_for_maxima(1, 0, first_s1[1][0])
            pe.wait_ge(max_done[0], 1)
            scores_for_maxima(1, 1, first_s1[1][1])
            pe.wait_ge(stack_kept, GROUPS)
            keep_clock(4)
            pe.wait_ge(max_split, 1)
            turn_max()
            pe.wait_ge(max_done[1], 1)
            scores_for_maxima(2, 0, first_s1[2][0])
            keep_clock(4)
            pe.wait_ge(max_done[0], 2)
            pe.wait_ge(q_max_ready, 1)
            scores_for_exp(0, 0)
            keep_clock(2)
            pe.wait_ge(max_done[1], 2)
            scores_for_maxima(2, 1, first_s1[2][1])
            pe.wait_ge(max_split, 2)
            turn_max()
            keep_clock(6)
            pe.wait_ge(max_done[0], 3)
            scores_for_exp(0, 1)

            def sequence(b, last_one):
                for g in range(GROUPS):
                    n = 4 * b + g
                    more = [not last_one or g + ahead < GROUPS for ahead in range(4)]
                    if more[1]:
                        pe.wait_ge(q_max_ready, n + 2)
                        pe.wait_ge(exp_done[0], after(n + 1))
                        scores_for_exp((g + 1) % GROUPS, 0)
                    if not last_one and g == 1:
                        pe.wait_ge(q_nat_ready, b + 2)
                        pe.wait_ge(k_nat_ready, b + 2)
                        stack_group(0, misc)
                    if more[1] and not more[3]:
                        pe.wait_ge(exp_done[1], after(n + 1))
                        scores_for_exp((g + 1) % GROUPS, 1)
                    if more[3] and g % 2 == 0:
                        pe.wait_ge(max_done[1], n + 3)
                        pe.wait_ge(stack_kept, n + 4)
                        scores_for_maxima((g + 3) % GROUPS, 0)
                    pe.wait_ge(pv_kept, after(n))
                    if g == 0:
                        pe.wait_ge(attn_done[1], after(b))
                    if g == 2 and not last_one:
                        pe.wait_ge(attn_done[0], after(b + 1))
                    if last_one and g == 2:
                        pe.wait_ge(q_max_ready, GROUPS * BATCH)
                        turn_values(0, in_misc)
                    if g % 2 == 0:
                        pe.wait_ge(v_ready[g // 2], b + 1)
                    pe.wait_ge(low_done[0], n + 1)
                    values(g, 0)
                    if more[3] and g % 2:
                        pe.wait_ge(max_done[1], n + 3)
                        pe.wait_ge(stack_kept, n + 4)
                        scores_for_maxima((g + 3) % GROUPS, 0)
                    if more[2]:
                        pe.wait_ge(max_split, n + 3)
                        pe.wait_ge(stack_kept, GROUPS * BATCH if last_one else n + 4)
                        turn_max()
                    if more[1] and more[3]:
                        pe.wait_ge(exp_done[1], after(n + 1))
                        scores_for_exp((g + 1) % GROUPS, 1)
                    pe.wait_ge(low_done[1], n + 1)
                    values(g, 1)
                    if more[3]:
                        pe.wait_ge(max_done[0], n + 4)
                        scores_for_maxima((g + 3) % GROUPS, 1)
                    if not last_one and g:
                        pe.wait_ge(q_max_ready, n + 3)
                        stack_group(g, misc)
                    if g % 2 and not last_one:
                        pe.wait_ge(pv_kept, after(n + 1))
                        turn_values(g // 2, by_sums)
                    if last_one and g == 2:
                        pe.wait_ge(attn_done[0], after(b + 1))
                        pe.wait_ge(x_norm_ready, 1)
                        turn_x(range(4))

            def gate(tiles):
                for t in tiles:
                    o = pv[:, 2 * t * EXPERTS:2 * (t + 1) * EXPERTS]
                    at = slice(t * P, (t + 1) * P)
                    nc.tensor.matmul(o, xh[:, at], gate_hl[:].rearrange("p a e -> p (a e)"),
                                     start=True, stop=False, skip_group_check=True)
                    last = nc.tensor.matmul(o[:, 0:EXPERTS], xl[:, at], gate_hl[:, 0, :],
                                            start=False, stop=True, skip_group_check=True)
                return last

            def up(k, base, pair):
                i, c, j = k // (CHUNKS * FT) % 2, k // FT % CHUNKS, k % FT
                n = k % UNITS
                turn = base + k // 2
                if c == 0 and j == 0 and k:
                    pe.wait_ge(w_split[i], after(3 * (pair + k // UNITS - 1 + i) + 1))
                xs = slice(c * CHUNK, (c + 1) * CHUNK)
                js = slice(j * P, (j + 1) * P)
                for m, ps in ((0, g_ps[n % 2]), (1, u_ps[n % 2])):
                    if m == 0:
                        pe.wait_ge(silu_done[n % 2], after(turn))
                    else:
                        if c == 0 and j == 0 and k:
                            pe.wait_ge(w_split[i], after(3 * (pair + k // UNITS - 1 + i) + 2))
                        pe.wait_ge(mul_done[n % 2], after(turn))
                    nc.tensor.matmul(ps, wh[i][m][:, js], xh[:, xs], start=True, stop=False)
                    nc.tensor.matmul(ps, wh[i][m][:, js], xl[:, xs], start=False, stop=False)
                    last = nc.tensor.matmul(ps, wl[i][m][:, js], xh[:, xs], start=False, stop=True)
                last.then_inc(up_done, 1)

            def down(k, pair):
                i, c, j = k // (CHUNKS * FT), k // FT % CHUNKS, k % FT
                if j == 0:
                    pe.wait_ge(scaled[c], after(2 * pair + i))
                    if c == 0:
                        pe.wait_ge(w_split[i], after(3 * (pair + i)))
                pe.wait_ge(hl_done[k % 4], after(UNITS // 4 * pair + k // 4 + 1))
                js = slice(j * P, (j + 1) * P)
                h, l = hh[k % 4][:], hl[k % 4][:]
                nc.tensor.matmul(d_ps[c], wh[i][2][:, js], h, start=j == 0, stop=False)
                nc.tensor.matmul(d_ps[c], wh[i][2][:, js], l, start=False, stop=False)
                nc.tensor.matmul(d_ps[c], wl[i][2][:, js], h, start=False,
                                 stop=j == FT - 1).then_inc(down_done[k % 4], 1)

            def turn_sums(c):
                pe.wait_ge(summed[c], after(EXPERTS))
                for t in range(CHUNK // P):
                    last = nc.tensor.transpose(banks[:, 6 + c, t * P:(t + 1) * P],
                                               acc[:, c, t * P:(t + 1) * P], ident)
                last.then_inc(y_turned, 1)

            with pe.Fori(0, LAST) as b:
                sequence(b, False)
            sequence(LAST, True)

            pe.wait_ge(w_first, 2)
            pe.wait_ge(xl_ready, 1)
            pe.wait_ge(exp_done[0], after(GROUPS * BATCH))
            up(0, 0, 0)
            pe.wait_ge(pv_kept, after(GROUPS * BATCH))
            turn_values(1, in_misc)
            up(1, 0, 0)
            pe.wait_ge(gate_ready, 1)
            gate(range(4))
            up(2, 0, 0)
            pe.wait_ge(attn_done[1], after(BATCH))
            pe.wait_ge(x_norm_ready, 2)
            turn_x(range(4, 8))
            up(3, 0, 0)
            pe.wait_ge(xl_ready, 2)
            gate(range(4, 8)).then_inc(logits_done, 1)
            pe.wait_ge(w_first, len(FIRST_WEIGHTS))
            with pe.Fori(0, PAIRS - 1) as pair:
                for k in range(UNITS):
                    up(k + LAG, UNITS // 2 * pair, pair)
                    down(k, pair)
            pair = PAIRS - 1
            for k in range(UNITS):
                if k + LAG < UNITS:
                    up(k + LAG, UNITS // 2 * pair, pair)
                down(k, pair)
            for c in range(CHUNKS):
                turn_sums(c)

        @block.scalar
        def _(act):
            for s in (*exp_done, pv_kept, *silu_done):
                act.sem_inc(s, 1)

            act.dma_start(cf[:], consts).then_inc(const_in, 16)
            act.wait_ge(k_loaded, 16)
            k_src = k_in[:].rearrange("p n (h c) -> p (n h) c", c=HEAD_DIM)
            nc.scalar.activation(k_rows[:, :, 2, :].bitcast(F32R), k_src, ACT.Copy)
            nc.scalar.activation(k_rows[:, :, 0, :].bitcast(F32R), k_src, ACT.Copy)
            act.wait_ge(const_in, 16)
            nc.scalar.activation(k_nat[:, :, QK_COLS:ROWS], k_const, ACT.Copy)\
                .then_inc(k_high, 1)

            def keep_stack(g, bank, count):
                act.wait_ge(stacked, count)
                nc.scalar.activation(qk_t[:, g].rearrange("p a t -> p (a t)"), bank,
                                     ACT.Copy).then_inc(stack_kept, 1)

            def exponentials(g, half, n):
                act.wait_ge(s2_done[half], n + 1)
                if not (isinstance(n, int) and n == 0):
                    act.wait_ge(low_done[half], n)
                    act.wait_ge(pv_done[half], after(n - 1))
                src = s2[half][:, :, 0:SCORE_COLS]
                nc.scalar.activation(probs[half][:], src, ACT.Exp)
                nc.scalar.activation(p_high[g % 2][half][:], src, ACT.Exp)\
                    .then_inc(exp_done[half], 1)

            for g, bank in enumerate((misc, banks[:, 2], banks[:, 3], banks[:, 4])):
                keep_stack(g, bank, g + 1)
            act.wait_ge(w_first_in, 48)
            for i, m in FIRST_WEIGHTS:
                nc.scalar.activation(wh[i][m][:], w_sb[m][:, i * FFN:(i + 1) * FFN], ACT.Copy)\
                    .then_inc(w_first_high, 1)
            for half in range(2):
                exponentials(0, half, 0)

            def keep_sums(g, b, n):
                act.wait_ge(pv_done[1], after(n + 1))
                act.wait_ge(pv_turned[g // 2], after(b))
                nc.scalar.activation(o_t[:, g, :], pv[0:VROWS, 0:SEQ], ACT.Copy)\
                    .then_inc(pv_kept, 1)

            def sequence(b, last_one):
                for g in range(GROUPS):
                    n = 4 * b + g
                    if last_one and g == GROUPS - 1:
                        keep_sums(g, b, n)
                    elif g % 2 and not last_one:
                        exponentials(g + 1, 0, n + 1)
                        keep_sums(g, b, n)
                        keep_stack(g, misc, n + GROUPS + 1)
                        exponentials(g + 1, 1, n + 1)
                    else:
                        exponentials(g + 1, 0, n + 1)
                        exponentials(g + 1, 1, n + 1)
                        keep_sums(g, b, n)
                    if not last_one and g % 2 == 0:
                        keep_stack(g, misc, n + GROUPS + 1)
                    if last_one and g == 2:
                        keep_x(0)

            def keep_x(piece):
                act.wait_ge(x_turned, piece + 1)
                lo, hi = X_PIECES[piece]
                nc.scalar.activation(xh[:, lo * P:hi * P], misc[:, 0:(hi - lo) * P],
                                     ACT.Copy).then_inc(xh_ready, 1)

            def silu_unit(k, pair):
                act.wait_ge(up_done, after(UNITS * pair + k + 1))
                act.wait_ge(mul_done[k % 2], after(UNITS // 2 * pair + k // 2))
                nc.scalar.activation(silu[k % 2][:], g_ps[k % 2], ACT.Silu)\
                    .then_inc(silu_done[k % 2], 1)

            def high_unit(k, pair):
                act.wait_ge(mul_done[k % 2], after(UNITS // 2 * pair + k // 2 + 1))
                act.wait_ge(down_done[k % 4], after(UNITS // 4 * pair + k // 4))
                nc.scalar.activation(hh[k % 4][:], hid[k % 2][:], ACT.Copy)\
                    .then_inc(hh_done[k % 4], 1)

            with act.Fori(0, LAST) as b:
                sequence(b, False)
            sequence(LAST, True)

            silu_unit(0, 0)
            silu_unit(1, 0)
            high_unit(0, 0)
            keep_x(1)
            silu_unit(2, 0)
            high_unit(1, 0)
            silu_unit(3, 0)
            high_unit(2, 0)
            silu_unit(4, 0)
            high_unit(3, 0)
            act.wait_ge(shifted, 1)
            nc.scalar.activation(prob[:], logits[:], ACT.Exp).then_inc(gate_exp, 1)
            with act.Fori(0, PAIRS - 1) as pair:
                for k in range(UNITS):
                    silu_unit(k + 5, pair)
                    high_unit(k + 4, pair)
            pair = PAIRS - 1
            for k in range(UNITS):
                if k + 5 < UNITS:
                    silu_unit(k + 5, pair)
                if k + 4 < UNITS:
                    high_unit(k + 4, pair)

        @block.gpsimd
        def _(pool):
            for s in (*hl_done, *summed):
                pool.sem_inc(s, 1)

            pool_steps = [0]

            def link(ins, base=0):
                pool_steps[0] += 1
                ins.then_inc(pool_chain, 1)
                pool.wait_ge(pool_chain, base + pool_steps[0])

            def none(n):
                return zeros[:, 0:n * HEAD_DIM].rearrange("p (n c) -> p n c", c=HEAD_DIM)

            k_src = k_in[:].rearrange("p n (h c) -> p (n h) c", c=HEAD_DIM)

            def low_keys():
                nc.gpsimd.tensor_tensor(k_rows[:, :, 1, :].bitcast(F32R), k_src,
                                        k_rows[:, :, 0, :], ALU.subtract).then_inc(k_nat_ready, 1)

            def keys(b, base):
                pool.wait_ge(k_loaded, 16 * b + 16)
                nc.gpsimd.tensor_tensor(k_rows[:, :, 2, :].bitcast(F32R), k_src,
                                        none(TPB * HEADS), ALU.add)
                link(nc.gpsimd.tensor_tensor(k_rows[:, :, 0, :].bitcast(F32R), k_src,
                                             none(TPB * HEADS), ALU.add), base)
                low_keys()

            def parts(t, grp, low):
                first = (t * HEADS + grp * HALF) * VROWS + (VHIGH if low else 0)
                flat = v_pad[:, first:first + 4 * (VROWS + VCOLS)]\
                    .rearrange("p (h c) -> p h c", c=VROWS + VCOLS)[:, :, 0:VCOLS]
                flat2 = v_pad[:, first + 4 * VROWS:first + 4 * VROWS + 4 * (VROWS + VCOLS)]\
                    .rearrange("p (h c) -> p h c", c=VROWS + VCOLS)[:, :, 0:VCOLS]
                return flat, flat2

            def value_columns(b, grp, base):
                pool.wait_ge(v_loaded, 16 * b + 16)
                for low in (False, True):
                    for t in range(TPB):
                        for i, dst in enumerate(parts(t, grp, low)):
                            at = (2 * grp + i) * 4 * HEAD_DIM
                            src = v_in[:, t, at:at + 4 * HEAD_DIM]\
                                .rearrange("p (h c) -> p h c", c=HEAD_DIM)
                            if low:
                                last = nc.gpsimd.tensor_tensor(
                                    dst[:, :, 0:HEAD_DIM], src,
                                    parts(t, grp, False)[i][:, :, 0:HEAD_DIM].bitcast(F32),
                                    ALU.subtract)
                            else:
                                last = nc.gpsimd.tensor_tensor(dst[:, :, 0:HEAD_DIM], src,
                                                               none(4), ALU.add)
                    if not low:
                        link(last, base)
                last.then_inc(v_ready[grp], 1)

            def low_probs(g, n):
                pool.wait_ge(exp_done[0], after(n + 1))
                nc.gpsimd.tensor_tensor(p_low[g % 2][0][:], probs[0][:],
                                        p_high[g % 2][0][:].bitcast(F32), ALU.subtract)\
                    .then_inc(low_done[0], 1)

            def low_first(n):
                i, m = FIRST_WEIGHTS[n]
                pool.wait_ge(w_first_high, n + 1)
                nc.gpsimd.tensor_tensor(wl[i][m][:], w_sb[m][:, i * FFN:(i + 1) * FFN],
                                        wh[i][m][:].bitcast(F32), ALU.subtract).then_inc(w_first, 1)

            def inverse_root(tiles, count):
                pool.wait_ge(var_ready, count)
                nc.gpsimd.tensor_tensor(rstd[:, tiles], veps[:, tiles], power[:, tiles], ALU.pow)\
                    .then_inc(rstd_ready, 1)

            nc.gpsimd.memset(power[:], -0.5)
            link(nc.gpsimd.memset(zeros[:], 0.0))
            nc.gpsimd.memset(v_pad[:].bitcast(F32), 0.0).then_inc(pool_chain, 1)
            pool_steps[0] += 1
            inverse_root(slice(0, TPB), 1)
            pool.wait_ge(k_high, 1)
            low_keys()
            pool.wait_ge(pool_chain, 2)
            for t in range(TPB):
                for grp in range(2):
                    for dst in parts(t, grp, False):
                        nc.gpsimd.memset(dst[:, :, HEAD_DIM:VCOLS].bitcast(F32), 1.0)
            inverse_root(slice(TPB, TILES), 2)
            value_columns(0, 0, 0)
            value_columns(0, 1, 0)
            for n in range(2):
                low_first(n)
            low_probs(0, 0)

            def sequence(b, last_one, base):
                for g in range(GROUPS):
                    n = 4 * b + g
                    if not last_one and g == 0:
                        pool.wait_ge(stacked, n + GROUPS)
                        keys(b + 1, base)
                    if not (last_one and g == GROUPS - 1):
                        low_probs(g + 1, n + 1)
                    if not last_one and g % 2:
                        pool.wait_ge(pv_done[1], after(n + 1))
                        value_columns(b + 1, g // 2, base)
                    if last_one and g == 1:
                        inverse_root(slice(0, TPB * LAST), 3)

            before = pool_steps[0]
            with pool.Fori(0, LAST) as b:
                pool_steps[0] = before
                sequence(b, False, 3 * b)
            assert pool_steps[0] == before + 3
            sequence(LAST, True, 0)
            for n in range(2, len(FIRST_WEIGHTS)):
                low_first(n)
            nc.gpsimd.memset(acc[:], 0.0)
            inverse_root(slice(TPB * LAST, TILES), 4)

            def low_unit(k, pair):
                pool.wait_ge(hh_done[k % 4], UNITS // 4 * pair + k // 4 + 1)
                pool.wait_ge(down_done[k % 4], after(UNITS // 4 * pair + k // 4))
                nc.gpsimd.tensor_tensor(hl[k % 4][:], hid[k % 2][:], hh[k % 4][:].bitcast(F32),
                                        ALU.subtract).then_inc(hl_done[k % 4], 1)

            def add_chunk(c, count):
                pool.wait_ge(scaled[c], after(count))
                pool.wait_ge(summed[c], after(count - 1))
                nc.gpsimd.tensor_tensor(acc[:, c, :], acc[:, c, :], part[c][:], ALU.add)\
                    .then_inc(summed[c], 1)

            def experts(pair, last_one):
                for k in range(UNITS):
                    if not (last_one and k + LAG + 2 >= UNITS - 2):
                        low_unit(k + LAG + 2, pair)
                    if k % FT == FT - 1 and not (last_one and k == UNITS - 1):
                        add_chunk(k // FT % CHUNKS, 2 * pair + k // (FT * CHUNKS) + 1)

            for k in range(LAG + 2):
                low_unit(k, 0)
            with pool.Fori(0, PAIRS - 1) as pair:
                experts(pair, False)
            experts(PAIRS - 1, True)

        @block.vector
        def _(dve):
            for s in (*attn_done, *mul_done, *scaled):
                dve.sem_inc(s, 1)

            steps = [0]

            def link(ins, base=0):
                steps[0] += 1
                ins.then_inc(dve_chain, 1)
                dve.wait_ge(dve_chain, base + steps[0])

            dve.sem_inc(w_split[0], 1)
            for _ in range(3):
                dve.sem_inc(w_split[1], 1)
            var = stats[:].rearrange("p (t c) -> p t c", c=2)[:, :, 1]

            def tile_sums(src, tiles, base):
                for t in tiles:
                    last = nc.vector.bn_stats(bn[:, t, :], src[:, t, :])
                link(last, base)

            def moments(tiles, scale, base):
                for t in tiles:
                    last = nc.vector.bn_aggr(stats[:, 2 * t:2 * t + 2], bn[:, t, :])
                link(last, base)
                at = slice(tiles[0], tiles[-1] + 1)
                nc.vector.tensor_scalar(veps[:, at], var[:, at], EPS, scale, ALU.add, ALU.mult)\
                    .then_inc(var_ready, 1)

            nc.vector.memset(max_nat[:], 0.0)
            dve.wait_ge(first_in, 16)
            tile_sums(x_in, range(0, TPB), 0)
            moments(range(0, TPB), float(HEAD_DIM), 0)
            dve.wait_ge(const_in, 16)
            nc.vector.tensor_copy(q_nat[:, :, QK_COLS:ROWS], q_const)
            nc.vector.tensor_copy(cb[:].rearrange("p a n -> p (a n)"), cf[:, 0:3 * P])\
                .then_inc(masks_ready, 1)
            dve.wait_ge(rstd_ready, 1)

            def x_normalised(tiles):
                for t in tiles:
                    last = nc.vector.tensor_scalar(x_norm[:, t, :], x_in[:, t, :],
                                                   stats[:, 2 * t:2 * t + 1], rstd[:, t:t + 1],
                                                   ALU.subtract, ALU.mult)
                return last

            def queries(b_next, base):
                src = x_norm[:, ds(TPB * b_next, TPB), :].rearrange("p n (h c) -> p (n h) c",
                                                                    c=HEAD_DIM)
                rows = q_nat[:, :, 0:QK_COLS].rearrange("p n (r c) -> p n r c", c=HEAD_DIM)
                link(nc.vector.tensor_copy(
                    rows[:, :, 0:2, :].bitcast(F32R),
                    src.unsqueeze(2).broadcast_to([P, TPB * HEADS, 2, HEAD_DIM])), base)
                nc.vector.tensor_tensor(rows[:, :, 2, :].bitcast(F32R), src, rows[:, :, 0, :],
                                        ALU.subtract).then_inc(q_nat_ready, 1)

            def maxima(half, count, s1=s1):
                if half == 0 and not (isinstance(count, int) and count == 1):
                    dve.wait_ge(max_split, count - 1)
                dve.wait_ge(s1_done[half], count)
                hs = slice(2 * half, 2 * half + 2)
                nc.vector.tensor_reduce(neg_max[:, 0, hs], s1[:, :, 0:P], AX.X, ALU.max,
                                        negate=True)
                return nc.vector.tensor_reduce(neg_max[:, 1, hs], s1[:, :, P:P + SEQ], AX.X,
                                               ALU.max, negate=True).then_inc(max_done[half], 1)

            def split_maxima(base, count):
                if not (isinstance(count, int) and count == 1):
                    dve.wait_ge(max_turned, count - 1)
                dve.wait_ge(max_done[0], count)
                dve.wait_ge(max_done[1], count)
                link(nc.vector.tensor_copy(max_nat[:, :, :, MAX_COL].bitcast(F32R), neg_max[:]),
                     base)
                nc.vector.tensor_tensor(max_nat[:, :, :, MAX_COL + 1].bitcast(F32R), neg_max[:],
                                        max_nat[:, :, :, MAX_COL], ALU.subtract)\
                    .then_inc(max_split, 1)

            def place_maxima(g, count):
                dve.wait_ge(max_turned, count)
                dve.wait_ge(stack_kept, count)
                nc.vector.tensor_tensor(q_max_t[:, g, :], misc[:, 0:SEQ],
                                        qk_t[:, g, 0, :].bitcast(F32), ALU.add)\
                    .then_inc(q_max_ready, 1)

            def finish_heads(b, grp, base, turned):
                dve.wait_ge(pv_turned[grp], after(b + 1))
                o = turned.rearrange("p t (h c) -> p t h c", c=VCOLS)
                link(nc.vector.reciprocal(r_den[:], o[:, :, :, HEAD_DIM]), base)
                nc.vector.tensor_tensor(
                    attn[:], o[:, :, :, 0:HEAD_DIM],
                    r_den[:].unsqueeze(3).broadcast_to([P, TPB, HALF, HEAD_DIM]), ALU.mult)\
                    .then_inc(attn_done[grp], 1)

            def add_residual(b, grp):
                dve.wait_ge(attn_done[grp], after(b + 1))
                cols = slice(grp * HALF * HEAD_DIM, (grp + 1) * HALF * HEAD_DIM)
                return nc.vector.tensor_tensor(
                    x_mid[:, ds(TPB * b, TPB), cols], attn[:].rearrange("p t h c -> p t (h c)"),
                    x_in[:, ds(TPB * b, TPB), cols], ALU.add)

            def low_probs(g, n):
                dve.wait_ge(exp_done[1], after(n + 1))
                nc.vector.tensor_tensor(p_low[g % 2][1][:], probs[1][:],
                                        p_high[g % 2][1][:].bitcast(F32), ALU.subtract)\
                    .then_inc(low_done[1], 1)

            link(x_normalised(range(TPB)))
            queries(0, 0)
            dve.wait_ge(rest_in, 16)
            tile_sums(x_in, range(TPB, TILES), 0)
            moments(range(TPB, TILES), float(HEAD_DIM), 0)
            for n in range(3):
                maxima(0, n + 1, first_s1[n][0])
                if n:
                    place_maxima(n - 1, n)
                else:
                    dve.wait_ge(rstd_ready, 2)
                    x_normalised(range(TPB, 4))
                maxima(1, n + 1, first_s1[n][1])
                x_normalised(range(4 + n, 5 + n))
                split_maxima(0, n + 1)
            link(x_normalised(range(7, TILES)))

            def x_mid_normalised(tiles, count):
                dve.wait_ge(rstd_ready, count)
                for t in tiles:
                    last = nc.vector.tensor_scalar(x_norm[:, t, :], x_mid[:, t, :],
                                                   stats[:, 2 * t:2 * t + 1], rstd[:, t:t + 1],
                                                   ALU.subtract, ALU.mult)
                    if t in (3, 7):
                        last.then_inc(x_norm_ready, 1)

            def low_x(piece):
                dve.wait_ge(xh_ready, piece + 1)
                lo, hi = X_PIECES[piece]
                nc.vector.tensor_tensor(xl[:, lo * P:hi * P], misc[:, 0:(hi - lo) * P],
                                        xh[:, lo * P:hi * P].bitcast(F32),
                                        ALU.subtract).then_inc(xl_ready, 1)

            def keep_logits():
                dve.wait_ge(logits_done, 1)
                sums = pv[:, 0:2 * TILES * EXPERTS].rearrange("p (t a e) -> p t a e", t=TILES, a=2)
                link(nc.vector.tensor_tensor(
                    logits[:], sums[:, :, 1],
                    bias_sb[:].unsqueeze(1).broadcast_to([P, TILES, EXPERTS]), ALU.add), base)
                nc.vector.tensor_tensor(logits[:], logits[:], sums[:, :, 0], ALU.add)\
                    .then_inc(logits_kept, 1)

            def sequence(b, last_one, per):
                base = per * b
                for g in range(GROUPS):
                    n = 4 * b + g
                    more = [not last_one or g + ahead < GROUPS for ahead in range(4)]
                    if not last_one and g == 0:
                        dve.wait_ge(stacked, 4 * b + GROUPS)
                    low_probs(g, n)
                    if last_one and g == 2:
                        x_mid_normalised(range(4), 3)
                    if last_one and g == 3:
                        low_x(0)
                        x_mid_normalised(range(4, TPB * LAST), 3)
                    if more[3]:
                        maxima(0, n + 4)
                    if more[2]:
                        place_maxima((g + 2) % GROUPS, n + 3)
                    if not last_one and g == 0:
                        queries(b + 1, base)
                    if last_one and g == 0:
                        dve.wait_ge(q_max_ready, n + 3)
                        tile_sums(x_mid, range(3), base)
                    if more[3]:
                        maxima(1, n + 4)
                        split_maxima(base, n + 4)
                    if not last_one and g % 2:
                        finish_heads(b, g // 2, base, by_sums)
                        last = add_residual(b, g // 2)
                    if last_one and g >= 2:
                        finish_heads(b, g - 2, base, in_misc)
                        last = add_residual(b, g - 2)
                    if last_one and g == 1:
                        tile_sums(x_mid, range(3, TPB * LAST), base)
                        moments(range(TPB * LAST), 1.0, base)
                        dve.wait_ge(gate_in, 32)
                        link(nc.vector.tensor_copy(gate_hl[:, 0, :], gate_sb[:]), base)
                        nc.vector.tensor_tensor(gate_hl[:, 1, :], gate_sb[:],
                                                gate_hl[:, 0, :].bitcast(F32),
                                                ALU.subtract).then_inc(gate_ready, 1)
                return last

            def multiply(k, pair):
                dve.wait_ge(silu_done[k % 2], after(UNITS // 2 * pair + k // 2 + 1))
                dve.wait_ge(hl_done[(k - 2) % 4],
                            after(UNITS // 4 * pair + (k - 2) // 4 + 1))
                nc.vector.tensor_tensor(hid[k % 2][:], silu[k % 2][:], u_ps[k % 2], ALU.mult)\
                    .then_inc(mul_done[k % 2], 1)

            before = steps[0]
            PER = 7
            with dve.Fori(0, LAST) as b:
                steps[0] = before
                sequence(b, False, PER)
            assert steps[0] - before == PER, steps[0] - before
            steps[0] = before
            base = PER * LAST
            link(sequence(LAST, True, PER), base)

            tile_sums(x_mid, range(TPB * LAST, TILES), base)
            moments(range(TPB * LAST, TILES), 1.0, base)
            multiply(0, 0)
            x_mid_normalised(range(TPB * LAST, TILES), 4)
            multiply(1, 0)
            low_x(1)
            multiply(2, 0)
            multiply(3, 0)
            keep_logits()
            dve.wait_ge(logits_kept, 1)

            def split_weights(i, m, e, count):
                src = w_sb[m][:, ds(e * FFN, FFN)]
                ins = nc.vector.tensor_copy(wh[i][m][:], src)
                ins.then_inc(w_high, 1)
                dve.wait_ge(w_high, count)
                nc.vector.tensor_tensor(wl[i][m][:], src, wh[i][m][:].bitcast(F32),
                                        ALU.subtract).then_inc(w_split[i], 1)

            link(nc.vector.tensor_reduce(row[:], logits[:], AX.X, ALU.max), base)
            nc.vector.tensor_tensor(logits[:], logits[:],
                                    row[:].unsqueeze(2).broadcast_to([P, TILES, EXPERTS]),
                                    ALU.subtract).then_inc(shifted, 1)
            multiply(4, 0)
            dve.wait_ge(gate_exp, 1)
            link(nc.vector.tensor_reduce(row[:], prob[:], AX.X, ALU.add), base)
            link(nc.vector.reciprocal(row[:], row[:]), base)
            link(nc.vector.tensor_tensor(prob[:], prob[:],
                                         row[:].unsqueeze(2).broadcast_to([P, TILES, EXPERTS]),
                                         ALU.mult), base)
            for t in range(TILES):
                last = nc.vector.max(top[:, t, :], prob[:, t, :])
            link(last, base)
            link(nc.vector.tensor_tensor(row[:], top[:, :, 0], top[:, :, 1], ALU.add), base)
            multiply(5, 0)
            link(nc.vector.memset(top[:, :, TOP_K:], -1.0), base)
            for t in range(TILES):
                nc.vector.match_replace(rest[:, t, :], top[:, t, :], prob[:, t, :], 0.0)
            link(nc.vector.reciprocal(row[:], row[:]), base)
            multiply(6, 0)
            link(nc.vector.tensor_tensor(prob[:], prob[:], rest[:], ALU.subtract), base)
            link(nc.vector.tensor_tensor(comb[:].rearrange("p e t -> p t e"), prob[:],
                                         row[:].unsqueeze(2).broadcast_to([P, TILES, EXPERTS]),
                                         ALU.mult), base)
            nc.vector.transpose(comb_t[:], comb[:].rearrange("p e t -> p (e t)"))\
                .then_inc(comb_turned, 1)

            def scale(k, pair):
                i, c = k // (CHUNKS * FT), k // FT % CHUNKS
                dve.wait_ge(down_done[k % 4], after(UNITS // 4 * pair + k // 4 + 1))
                dve.wait_ge(comb_in[i], 16 * (pair + 1))
                dve.wait_ge(summed[c], after(2 * pair + i))
                nc.vector.tensor_tensor(part[c][:], d_ps[c],
                                        comb_all[i][:, c * CHUNK:(c + 1) * CHUNK], ALU.mult)\
                    .then_inc(scaled[c], 1)

            def low_last(k):
                dve.wait_ge(hh_done[k % 4], UNITS // 4 * PAIRS)
                dve.wait_ge(down_done[k % 4], after(UNITS // 4 * PAIRS - 1))
                nc.vector.tensor_tensor(hl[k % 4][:], hid[k % 2][:], hh[k % 4][:].bitcast(F32),
                                        ALU.subtract).then_inc(hl_done[k % 4], 1)

            def add_last(c):
                dve.wait_ge(scaled[c], after(EXPERTS))
                dve.wait_ge(summed[c], after(EXPERTS - 1))
                nc.vector.tensor_tensor(acc[:, c, :], acc[:, c, :], part[c][:], ALU.add)\
                    .then_inc(summed[c], 1)

            def experts(pair, last_one):
                count = 6 * pair
                for k in range(UNITS):
                    if not (last_one and k + LAG + 3 >= UNITS):
                        multiply(k + LAG + 3, pair)
                    if k == 1:
                        dve.wait_ge(down_done[3], after(UNITS // 4 * pair))
                        split_weights(1, 2, 2 * pair + 1, count + 1)
                    if not last_one and k in (5, 6):
                        dve.wait_ge(up_done, after(UNITS * pair + UNITS // 2))
                        split_weights(0, k - 5, 2 * pair + 2, count + k - 3)
                    if not last_one and k == 9:
                        dve.wait_ge(down_done[3], after(UNITS // 4 * pair + UNITS // 8))
                        split_weights(0, 2, 2 * pair + 2, count + 4)
                    if not last_one and k in (12, 13):
                        dve.wait_ge(up_done, after(UNITS * pair + UNITS))
                        split_weights(1, k - 12, 2 * pair + 3, count + k - 7)
                    if last_one and k == UNITS - FT - 1:
                        low_last(UNITS - 2)
                        low_last(UNITS - 1)
                    if k % FT == FT - 1:
                        scale(k, pair)

            dve.wait_ge(w_first_in, 48)
            dve.wait_ge(w_in, 48)
            with dve.Fori(0, PAIRS - 1) as pair:
                experts(pair, False)
            experts(PAIRS - 1, True)
            add_last(CHUNKS - 1)

            half = TILES // 2
            for c in range(CHUNKS):
                dve.wait_ge(y_turned, c + 1)
                nc.vector.tensor_tensor(
                    y[:, c * half:(c + 1) * half, :].rearrange("p t d -> p (t d)"),
                    banks[:, 6 + c, :],
                    x_mid[:, c * half:(c + 1) * half, :].rearrange("p t d -> p (t d)"),
                    ALU.add).then_inc(y_ready, 1)


_INS = ["x", "ctx_1024", "L0_ffn_gate_w", "L0_ffn_gate_b", "L0_ffn_w1", "L0_ffn_w3", "L0_ffn_w2"]


def kernel(**inputs):
    import concourse.bacc as bacc
    from concourse.bass_utils import run_bass_kernel_spmd

    nc = bacc.Bacc("TRN2", target_bir_lowering=False, num_devices=1)
    arrays = {name: np.ascontiguousarray(inputs[name]) for name in _INS}
    for name in ("x", "ctx_1024", "L0_ffn_w2"):
        arrays[name] = arrays[name].reshape(-1, D)
    arrays["consts"] = constants()
    arrays = {f"in_{name}": a for name, a in arrays.items()}
    args = [nc.dram_tensor(name, a.shape, mybir.dt.from_np(a.dtype), kind="ExternalInput").ap()
            for name, a in arrays.items()]
    out = nc.dram_tensor("out", (TOKENS, D), mybir.dt.float32, kind="ExternalOutput").ap()
    c_dram = nc.dram_tensor("c_dram", (EXPERTS * TILES, P), mybir.dt.float32, kind="Internal").ap()
    build(nc, *args, out, c_dram)
    r = run_bass_kernel_spmd(nc, [arrays], core_ids=[0])
    return r.results[0]["out"].reshape(BATCH, SEQ, D)
```
